# Optimizing a Trainium2 kernel written in Bass

```python
import numpy as np
import jax
import jax.numpy as jnp

def _softmax(x, axis=-1):
    return jax.nn.softmax(x, axis=axis)

def _gelu(x):
    return jax.nn.gelu(x, approximate=True)

def _silu(x):
    return jax.nn.silu(x)

def _sigmoid(x):
    return jax.nn.sigmoid(x)

def _layernorm(x, axis=-1, eps=1e-05):
    m = jnp.mean(x, axis=axis, keepdims=True)
    v = jnp.var(x, axis=axis, keepdims=True)
    return (x - m) / jnp.sqrt(v + eps)

def _scatter_add(tgt, idx, src, axis=0):
    return tgt.at[idx].add(src)

def _segment_sum(src, seg, n):
    return jax.ops.segment_sum(src, seg, n)
kernel_name = 'mk_adj_resnorm_d1_adj_r2_60206b'

def setup_inputs(seed: int=0):
    np.random.seed(seed)
    _w = jnp.asarray

    def _rec_inputs():
        import jax
        import jax.numpy as jnp
        _gk = jax.random.key(seed)
        x = 7.22e-05 + 1 * jax.random.normal(jax.random.fold_in(_gk, 1), (128, 128, 256), jnp.float32)
        _a = jax.random.bernoulli(jax.random.fold_in(_gk, 2), 0.125, (128, 128, 128))
        _a = jnp.logical_or(_a, jnp.swapaxes(_a, -1, -2))
        _a = jnp.logical_or(_a, jnp.eye(128, dtype=bool))
        _af = _a.astype(jnp.float32)
        _af = _af * jax.random.uniform(jax.random.fold_in(_gk, 3), (128, 128, 128), jnp.float32, 0.05, 1)
        adj = _af
        return (x, adj)
    x, adj = _rec_inputs()

    def _L0_gnn_setup():
        import jax, jax.numpy as jnp
        import numpy as np
        EPS_LN = 1e-05

        def hypergraph_conv(x, adj, W, b):
            N, C, _ = adj.shape
            H = (adj != 0).astype(x.dtype)
            w = adj.reshape(N, -1)[:, :C]
            xw = jnp.einsum('ncd,hd->nch', x, W)
            Dn = jnp.einsum('nce,ne->nc', H, w)
            Dn = jnp.where(Dn > 0, 1.0 / Dn, 0.0)
            Be = H.sum(axis=1)
            Be = jnp.where(Be > 0, 1.0 / Be, 0.0)
            m = Be[:, :, None] * jnp.einsum('nce,nch->neh', H, xw)
            out = Dn[:, :, None] * jnp.einsum('nce,neh->nch', H, m)
            return out + b

        def layer_norm(x, g, b):
            mu = jnp.mean(x, axis=-1, keepdims=True)
            var = jnp.var(x, axis=-1, keepdims=True)
            return (x - mu) * jax.lax.rsqrt(var + EPS_LN) * g + b
        key = jax.random.key(seed)
        ks = jax.random.split(key, 4)
        N, C, Din, Dh, Dout = (16, 512, 256, 512, 256)
        x = jax.random.normal(ks[0], (N, C, Din), dtype=jnp.float32)
        adj = jax.random.uniform(ks[1], (N, C, C), dtype=jnp.float32, minval=0.1, maxval=1.0)
        W1 = jax.random.normal(ks[2], (Dh, Din), dtype=jnp.float32) * (1.0 / np.sqrt(Din))
        b1 = jnp.zeros((Dh,), dtype=jnp.float32)
        gamma = jnp.ones((Dh,), dtype=jnp.float32)
        beta = jnp.zeros((Dh,), dtype=jnp.float32)
        W2 = jax.random.normal(ks[3], (Dout, Dh), dtype=jnp.float32) * (1.0 / np.sqrt(Dh))
        b2 = jnp.zeros((Dout,), dtype=jnp.float32)
        return {'x': x, 'adj': adj, 'W1': W1, 'b1': b1, 'gamma': gamma, 'beta': beta, 'W2': W2, 'b2': b2}
    _L0_gnn_all = _L0_gnn_setup()
    _L0_gnn_in = {k: v for k, v in _L0_gnn_all.items() if k in ('W1', 'b1', 'gamma', 'beta', 'W2', 'b2')}
    del _L0_gnn_all
    return {'x': x, 'adj': adj, 'L0_gnn_W1': _L0_gnn_in['W1'], 'L0_gnn_b1': _L0_gnn_in['b1'], 'L0_gnn_gamma': _L0_gnn_in['gamma'], 'L0_gnn_beta': _L0_gnn_in['beta'], 'L0_gnn_W2': _L0_gnn_in['W2'], 'L0_gnn_b2': _L0_gnn_in['b2']}

def reference(x, adj, L0_gnn_W1, L0_gnn_b1, L0_gnn_gamma, L0_gnn_beta, L0_gnn_W2, L0_gnn_b2):
    import jax
    import jax.numpy as jnp

    def _L0_gnn_ref(x, adj, W1, b1, gamma, beta, W2, b2):
        import jax, jax.numpy as jnp
        import numpy as np
        EPS_LN = 1e-05

        def hypergraph_conv(x, adj, W, b):
            N, C, _ = adj.shape
            H = (adj != 0).astype(x.dtype)
            w = adj.reshape(N, -1)[:, :C]
            xw = jnp.einsum('ncd,hd->nch', x, W)
            Dn = jnp.einsum('nce,ne->nc', H, w)
            Dn = jnp.where(Dn > 0, 1.0 / Dn, 0.0)
            Be = H.sum(axis=1)
            Be = jnp.where(Be > 0, 1.0 / Be, 0.0)
            m = Be[:, :, None] * jnp.einsum('nce,nch->neh', H, xw)
            out = Dn[:, :, None] * jnp.einsum('nce,neh->nch', H, m)
            return out + b

        def layer_norm(x, g, b):
            mu = jnp.mean(x, axis=-1, keepdims=True)
            var = jnp.var(x, axis=-1, keepdims=True)
            return (x - mu) * jax.lax.rsqrt(var + EPS_LN) * g + b
        h = jax.nn.relu(hypergraph_conv(x, adj, W1, b1))
        h = layer_norm(h, gamma, beta)
        y = hypergraph_conv(h, adj, W2, b2)
        return y + x
    x = _layernorm(x + _L0_gnn_ref(x, adj, L0_gnn_W1, L0_gnn_b1, L0_gnn_gamma, L0_gnn_beta, L0_gnn_W2, L0_gnn_b2), axis=-1)
    return x

_drawn_inputs = setup_inputs


def setup_inputs(seed=0):
    import zlib

    import numpy as np

    out = dict(_drawn_inputs(seed))
    spreads = {'L0_gnn_b1': (0.0, 0.1),
     'L0_gnn_gamma': (1.0, 0.2),
     'L0_gnn_beta': (0.0, 0.1),
     'L0_gnn_b2': (0.0, 0.545)}
    factors = {}
    for name, (base, spread) in spreads.items():
        noise = np.random.default_rng([zlib.crc32(name.encode()), seed]).standard_normal(out[name].shape)
        drawn = base * np.exp(spread * noise) if base else spread * noise
        out[name] = jnp.asarray(drawn.astype(out[name].dtype))
    for name, factor in factors.items():
        out[name] = (out[name] * factor).astype(out[name].dtype)
    return out
```

```python
import concourse.bass as bass
from concourse import mybir
from contextlib import ExitStack

F32 = mybir.dt.float32
F32R = mybir.dt.float32r
BF16 = mybir.dt.bfloat16
ALU = mybir.AluOpType
ACT = mybir.ActivationFunctionType
AX = mybir.AxisListType

P = 128
LN_EPS = 1e-5
TINY = 1.1754944e-38


def hypergraph_block(nc, x, adj, w1, b1, gamma, beta, w2, b2, out):
    graphs, nodes, d_in = x.shape
    d_hid = w1.shape[0]
    assert nodes == P and d_in == w2.shape[0]
    DB = d_in // P
    HB = d_hid // P
    G4 = 512 // P
    GROUPS = graphs // G4
    PAIRS = GROUPS // 2

    ctx = ExitStack()
    with ctx:
        def sb(name, shape, dt=F32):
            return ctx.enter_context(nc.sbuf_tensor(name, shape, dt))

        def sem(name):
            return ctx.enter_context(nc.semaphore(name))

        ident = sb("ident", [P, P])
        ident_bf = sb("ident_bf", [P, P], BF16)
        ones_row = sb("ones_row", [1, P])
        ones_sq = sb("ones_sq", [P, P])
        ones_bf = sb("ones_bf", [P, 1], BF16)
        minus_half = sb("minus_half", [P, 2])
        eps = sb("eps", [P, 2])
        w1_rows = sb("w1_rows", [P, HB, d_in])
        w2_rows = sb("w2_rows", [P, DB, d_hid])
        w2_scaled = sb("w2_scaled", [P, DB, d_hid])
        w2_centred = sb("w2_centred", [P, DB, d_hid])
        w2_beta = sb("w2_beta", [P, DB, d_hid])
        gamma_row = sb("gamma_row", [1, d_hid])
        beta_row = sb("beta_row", [1, d_hid])
        b1_row = sb("b1_row", [1, d_hid])
        b2_row = sb("b2_row", [1, d_in])
        first_rows = sb("first_rows", [P, P])
        w2_sum = sb("w2_sum", [P, DB])
        w2_mean = sb("w2_mean", [P, DB])
        t_col = sb("t_col", [P, DB])
        t_wide = sb("t_wide", [P, DB, P])
        b1_col = sb("b1_col", [P, HB])
        b2_half = sb("b2_half", [P, 2, d_in])
        t_all = sb("t_all", [P, d_in])
        edge_w = sb("edge_w", [P, graphs])
        w1_hi = sb("w1_hi", [P, DB, d_hid], F32R)
        w1_lo = sb("w1_lo", [P, DB, d_hid], F32R)
        w2_hi = sb("w2_hi", [P, HB, d_in], F32R)
        w2_lo = sb("w2_lo", [P, HB, d_in], F32R)

        adj_sb = sb("adj_sb", [P, 2, G4, P])
        x_sb = sb("x_sb", [P, 2, G4, d_in])
        xb_sb = sb("xb_sb", [P, 2, G4, d_in])
        at_sb = sb("at_sb", [P, 2, G4, P])
        out_sb = sb("out_sb", [P, 2, G4, d_in])
        inc_bf = sb("inc_bf", [P, G4, P], BF16)
        inc_t = sb("inc_t", [P, G4, P])
        safe = sb("safe", [P, 2 * G4])
        inv = sb("inv", [P, 2 * G4])
        d_pos = sb("d_pos", [P, G4])
        d_inv = sb("d_inv", [P, G4])
        scaled = sb("scaled", [P, G4, P])
        scaled_t = sb("scaled_t", [P, G4, P])
        u_hi = sb("u_hi", [P, DB, G4 * P], F32R)
        u_lo = sb("u_lo", [P, DB, G4 * P], F32R)
        h_sb = sb("h_sb", [P, HB, G4 * P])
        h_hi = sb("h_hi", [P, HB, G4 * P], F32R)
        h_lo = sb("h_lo", [P, HB, G4 * P], F32R)
        v_sb = sb("v_sb", [P, G4, d_in])
        z_sb = sb("z_sb", [P, G4, d_in])
        h_stats = sb("h_stats", [P, G4, 6])
        h_mv = sb("h_mv", [P, G4, 2])
        h_var = sb("h_var", [P, G4])
        h_rstd = sb("h_rstd", [P, G4])
        z_stats = sb("z_stats", [P, G4, 6])
        z_mv = sb("z_mv", [P, G4, 2])
        z_var = sb("z_var", [P, G4])
        z_rstd = sb("z_rstd", [P, G4])

        bank = [ctx.enter_context(nc.psum_tensor(f"bank{i}", [P, 512], F32)) for i in range(8)]
        ps_hid = bank[0:2]
        ps_v = bank[2:4]
        ps_ht = bank[4:6]
        ps_adj = bank[6]
        ps_y = bank[7]

        rows_in = sem("rows_in")
        w_in = sem("w_in")
        adj_in = [sem(f"adj_in{p}") for p in range(2)]
        x_in = [sem(f"x_in{p}") for p in range(2)]
        stored = [sem(f"stored{p}") for p in range(2)]
        zeroed = sem("zeroed")
        consts = sem("consts")
        rows_spread = sem("rows_spread")
        w1_turned = sem("w1_turned")
        edge_turned = sem("edge_turned")
        w2_prep = sem("w2_prep")
        w2_turned = sem("w2_turned")
        t_spread = sem("t_spread")
        set_hi = sem("set_hi")
        set_up = sem("set_up")
        inc_turned = sem("inc_turned")
        sums_done = sem("sums_done")
        scaled_turned = sem("scaled_turned")
        at_done = sem("at_done")
        u_done = sem("u_done")
        hid_done = sem("hid_done")
        ht_done = sem("ht_done")
        v_done = sem("v_done")
        y_done = sem("y_done")
        inc_t_ready = sem("inc_t_ready")
        scaled_t_ready = sem("scaled_t_ready")
        at_ready = sem("at_ready")
        u_hi_ready = sem("u_hi_ready")
        h_hi_ready = sem("h_hi_ready")
        inc_ready = sem("inc_ready")
        sums_safe = sem("sums_safe")
        inv_ready = sem("inv_ready")
        d_inv_ready = sem("d_inv_ready")
        scaled_ready = sem("scaled_ready")
        u_lo_ready = sem("u_lo_ready")
        h_lo_ready = sem("h_lo_ready")
        h_stats_ready = sem("h_stats_ready")
        stats_seen = sem("stats_seen")
        h_mv_ready = sem("h_mv_ready")
        v_ready = sem("v_ready")
        z_ready = sem("z_ready")
        z_stats_ready = sem("z_stats_ready")
        z_mv_ready = sem("z_mv_ready")
        out_ready = sem("out_ready")
        xb_ready = sem("xb_ready")
        h_eps = sem("h_eps")
        h_rstd_ready = sem("h_rstd_ready")
        z_eps = sem("z_eps")
        z_rstd_ready = sem("z_rstd_ready")

        adj_dram = adj.rearrange("n i e -> i n e")
        x_dram = x.rearrange("n c d -> c n d")
        out_dram = out.rearrange("n c d -> c n d")

        def wait(eng, s, value):
            if not isinstance(value, int) or value > 0:
                eng.wait_ge(s, value)

        def grp(k, off):
            return 2 * k + off

        def graph0(k, off):
            return 2 * G4 * k + G4 * off

        def loads(k, off):
            return 16 * k + 16 * (off // 2 + 1)

        def over_groups(eng, iteration):
            iteration(0, 0, True, False)
            iteration(0, 1, False, False)
            with eng.Fori(1, PAIRS - 1) as k:
                for off in range(2):
                    iteration(k, off, False, False)
            iteration(PAIRS - 1, 0, False, False)
            iteration(PAIRS - 1, 1, False, True)

        block = ctx.enter_context(nc.Block())

        @block.sync
        def _(sp):
            def load_adj(k, off):
                sp.dma_start(adj_sb[:, off % 2], adj_dram[:, bass.ds(graph0(k, off), G4)]
                             ).then_inc(adj_in[off % 2], 16)

            def load_x(k, off):
                sp.dma_start(x_sb[:, off % 2], x_dram[:, bass.ds(graph0(k, off), G4)]
                             ).then_inc(x_in[off % 2], 16)

            def store(k, off):
                wait(sp, out_ready, G4 * (grp(k, off) + 1))
                sp.dma_start(out_dram[:, bass.ds(graph0(k, off), G4)], out_sb[:, off % 2]
                             ).then_inc(stored[off % 2], 16)

            load_adj(0, 0)
            sp.dma_start(gamma_row[:, :], gamma.rearrange("(a n) -> a n", a=1)).then_inc(rows_in, 16)
            sp.dma_start(beta_row[:, :], beta.rearrange("(a n) -> a n", a=1)).then_inc(rows_in, 16)
            sp.dma_start(b1_row[:, :], b1.rearrange("(a n) -> a n", a=1)).then_inc(rows_in, 16)
            sp.dma_start(b2_row[:, :], b2.rearrange("(a n) -> a n", a=1)).then_inc(rows_in, 16)
            sp.dma_start(first_rows[:, :], adj[:, 0, :]).then_inc(w_in, 16)
            sp.dma_start(w1_rows[:, :, :], w1.rearrange("(b p) d -> p b d", p=P)).then_inc(w_in, 16)
            sp.dma_start(w2_rows[:, :, :], w2.rearrange("(b p) h -> p b h", p=P)).then_inc(w_in, 16)
            load_x(0, 0)
            load_adj(0, 1)
            load_x(0, 1)

            def iteration(k, off, first, last):
                g = grp(k, off)
                if not (last or (off == 0 and isinstance(k, int) and k == PAIRS - 1)):
                    wait(sp, scaled_ready, g + 1)
                    load_adj(k, off + 2)
                    wait(sp, u_done, DB * (g + 1))
                    wait(sp, xb_ready, 2 * (g + 1))
                    load_x(k, off + 2)
                if not first:
                    store(k, off - 1)

            over_groups(sp, iteration)
            store(PAIRS - 1, 1)
            for p in range(2):
                sp.wait_ge(stored[p], 16 * PAIRS)

        @block.gpsimd
        def _(pool):
            nc.gpsimd.memset(ident[:, :], 0.0).then_inc(zeroed, 1)
            nc.gpsimd.memset(ident_bf[:, :], 0.0).then_inc(zeroed, 1)
            nc.gpsimd.memset(ones_row[:, :], 1.0)
            nc.gpsimd.memset(ones_sq[:, :], 1.0)
            nc.gpsimd.memset(ones_bf[:, :], 1.0)
            nc.gpsimd.memset(minus_half[:, :], -0.5)
            nc.gpsimd.memset(eps[:, :], LN_EPS)
            pool.wait_ge(zeroed, 2)
            for m in (ident, ident_bf):
                nc.gpsimd.affine_select(out=m[:, :], in_=m[:, :], compare_op=ALU.not_equal, fill=1.0,
                                        base=0, pattern=[[-1, P]], channel_multiplier=1).then_inc(consts, 1)

            def residual(k, off):
                g, p = grp(k, off), off % 2
                wait(pool, x_in[p], loads(k, off))
                wait(pool, z_ready, 2 * (g - 1))
                for q in range(2):
                    nc.gpsimd.tensor_tensor(xb_sb[:, p, 2 * q:2 * q + 2], x_sb[:, p, 2 * q:2 * q + 2],
                                            b2_half[:, :, :], ALU.add).then_inc(xb_ready, 1)

            def rstd(k, off, q, mv, mv_ready, var, eps_done, r, r_ready):
                n = 2 * grp(k, off) + q
                cols = slice(2 * q, 2 * q + 2)
                wait(pool, mv_ready, 2 * n + 2)
                nc.gpsimd.tensor_tensor(var[:, cols], mv[:, cols, 1], eps[:, :], ALU.add
                                        ).then_inc(eps_done, 1)
                wait(pool, eps_done, n + 1)
                nc.gpsimd.tensor_tensor(r[:, cols], var[:, cols], minus_half[:, :], ALU.pow
                                        ).then_inc(r_ready, 1)

            def h_scale(k, off, q):
                wait(pool, v_ready, G4 * (grp(k, off) - 1) + 2 * q + 2)
                rstd(k, off, q, h_mv, h_mv_ready, h_var, h_eps, h_rstd, h_rstd_ready)

            def z_scale(k, off, q):
                wait(pool, out_ready, G4 * (grp(k, off) - 1) + 2 * q + 2)
                rstd(k, off, q, z_mv, z_mv_ready, z_var, z_eps, z_rstd, z_rstd_ready)

            pool.wait_ge(set_up, 2)
            residual(0, 0)

            def iteration(k, off, first, last):
                if not first:
                    h_scale(k, off - 1, 1)
                    z_scale(k, off - 1, 0)
                    z_scale(k, off - 1, 1)
                if not last:
                    residual(k, off + 1)
                h_scale(k, off, 0)

            over_groups(pool, iteration)
            h_scale(PAIRS - 1, 1, 1)
            z_scale(PAIRS - 1, 1, 0)
            z_scale(PAIRS - 1, 1, 1)

        @block.scalar
        def _(act):
            def h_block(k, off, hb):
                g = grp(k, off)
                wait(act, hid_done, HB * g + hb + 1)
                if hb == 0:
                    wait(act, v_done, G4 * g)
                    wait(act, ht_done, G4 * g)
                    wait(act, h_lo_ready, HB * g)
                nc.scalar.activation(h_sb[:, hb], ps_hid[hb % 2][:, :], ACT.Relu, bias=b1_col[:, hb:hb + 1])
                nc.scalar.activation(h_hi[:, hb], ps_hid[hb % 2][:, :], ACT.Relu, bias=b1_col[:, hb:hb + 1]
                                     ).then_inc(h_hi_ready, 1)

            def copy_inc_t(k, off):
                g = grp(k, off)
                wait(act, inc_turned, g + 1)
                wait(act, at_done, g)
                nc.scalar.activation(inc_t[:, :, :], ps_adj[:, 0:256].bitcast(BF16), ACT.Copy
                                     ).then_inc(inc_t_ready, 1)

            def scale_t(k, off):
                g = grp(k, off)
                wait(act, scaled_turned, g + 1)
                wait(act, at_done, g)
                for j in range(G4):
                    nc.scalar.activation(scaled_t[:, j], ps_adj[:, j * P:(j + 1) * P], ACT.Copy,
                                         scale=inv[:, j:j + 1]).then_inc(scaled_t_ready, 1)

            def copy_at(k, off):
                g = grp(k, off)
                wait(act, at_done, g + 1)
                wait(act, y_done, 2 * (g - 1))
                nc.scalar.activation(at_sb[:, off % 2], ps_adj[:, :], ACT.Copy).then_inc(at_ready, 1)

            def u_high(k, off):
                g = grp(k, off)
                wait(act, hid_done, HB * g)
                for db in range(DB):
                    wait(act, u_done, DB * g + db + 1)
                    nc.scalar.activation(u_hi[:, db], ps_hid[db][:, :], ACT.Copy).then_inc(u_hi_ready, 1)

            act.wait_ge(edge_turned, 1)
            nc.scalar.activation(edge_w[:, :], bank[5][:, 0:graphs], ACT.Copy).then_inc(set_hi, 1)
            act.wait_ge(w1_turned, 1)
            for db in range(DB):
                nc.scalar.activation(w1_hi[:, db], bank[3 + db][:, :], ACT.Copy).then_inc(set_hi, 1)
            act.wait_ge(w2_turned, 1)
            for i in range(2):
                nc.scalar.activation(w2_hi[:, 2 * i:2 * i + 2], bank[i][:, :], ACT.Copy).then_inc(set_hi, 1)
            act.wait_ge(set_up, 3)

            copy_inc_t(0, 0)
            scale_t(0, 0)
            copy_at(0, 0)
            u_high(0, 0)

            def iteration(k, off, first, last):
                for hb in range(HB):
                    if hb == 3 and not last:
                        copy_inc_t(k, off + 1)
                    h_block(k, off, hb)
                if not last:
                    scale_t(k, off + 1)
                    copy_at(k, off + 1)
                    u_high(k, off + 1)

            over_groups(act, iteration)

        @block.vector
        def _(dve):
            def incidence(k, off):
                g, p = grp(k, off), off % 2
                wait(dve, adj_in[p], loads(k, off))
                wait(dve, inc_turned, g)
                wait(dve, sums_done, g)
                nc.vector.tensor_scalar(inc_bf[:, :, :], adj_sb[:, p], 0.0, None, ALU.not_equal
                                        ).then_inc(inc_ready, 1)

            def inverses(k, off):
                g, p = grp(k, off), off % 2
                wait(dve, sums_done, g + 1)
                wait(dve, scaled_t_ready, G4 * g)
                wait(dve, scaled_ready, g)
                nc.vector.tensor_scalar(safe[:, 0:G4], ps_adj[:, 0:G4], 1.0, None, ALU.max).then_inc(sums_safe, 1)
                nc.vector.tensor_scalar(safe[:, G4:2 * G4], ps_adj[:, G4:2 * G4], TINY, None, ALU.max
                                        ).then_inc(sums_safe, 1)
                nc.vector.tensor_scalar(d_pos[:, :], ps_adj[:, G4:2 * G4], 0.0, None, ALU.is_gt
                                        ).then_inc(sums_safe, 1)
                wait(dve, sums_safe, 3 * g + 3)
                nc.vector.reciprocal(inv[:, :], safe[:, :]).then_inc(inv_ready, 1)
                wait(dve, inv_ready, g + 1)
                nc.vector.tensor_tensor(d_inv[:, :], inv[:, G4:2 * G4], d_pos[:, :], ALU.mult
                                        ).then_inc(d_inv_ready, 1)
                wait(dve, d_inv_ready, g + 1)
                for j in range(G4):
                    last = nc.vector.tensor_scalar(scaled[:, j], adj_sb[:, p, j], 0.0, d_inv[:, j:j + 1],
                                                   ALU.not_equal, ALU.mult)
                last.then_inc(scaled_ready, 1)

            def u_low(k, off):
                g = grp(k, off)
                for db in range(DB):
                    wait(dve, u_hi_ready, DB * g + db + 1)
                    nc.vector.tensor_tensor(u_lo[:, db], ps_hid[db][:, :], u_hi[:, db].bitcast(F32),
                                            ALU.subtract).then_inc(u_lo_ready, 1)

            def h_low(k, off, hb):
                g = grp(k, off)
                wait(dve, h_hi_ready, HB * g + hb + 1)
                nc.vector.tensor_tensor(h_lo[:, hb], h_sb[:, hb], h_hi[:, hb].bitcast(F32),
                                        ALU.subtract).then_inc(h_lo_ready, 1)

            def h_variance(k, off, b):
                n = G4 * grp(k, off) + b
                wait(dve, ht_done, n + 1)
                wait(dve, h_rstd_ready, 2 * (grp(k, off) - 1) + b // 2 + 1)
                nc.vector.bn_stats(h_stats[:, b], ps_ht[b % 2][:, :]).then_inc(h_stats_ready, 1)
                wait(dve, h_stats_ready, n + 1)
                dve.sem_inc(stats_seen, 1)
                nc.vector.bn_aggr(h_mv[:, b], h_stats[:, b]).then_inc(h_mv_ready, 1)

            def v_rows(k, off, q):
                g = grp(k, off)
                wait(dve, h_rstd_ready, 2 * g + q + 1)
                wait(dve, v_done, G4 * g + 2 * q + 2)
                for b in (2 * q, 2 * q + 1):
                    nc.vector.scalar_tensor_tensor(v_sb[:, b], ps_v[q][:, (b % 2) * d_in:(b % 2 + 1) * d_in],
                                                   h_rstd[:, b:b + 1], t_all[:, :], ALU.mult, ALU.add
                                                   ).then_inc(v_ready, 1)

            def z_rows(k, off, q):
                g, p, n = grp(k, off), off % 2, 2 * grp(k, off) + q
                wait(dve, y_done, n + 1)
                wait(dve, xb_ready, n + 1)
                wait(dve, out_ready, G4 * (g - 1) + 2 * q + 2)
                nc.vector.scalar_tensor_tensor(z_sb[:, 2 * q:2 * q + 2].rearrange("p a d -> p (a d)"),
                                               xb_sb[:, p, 2 * q:2 * q + 2].rearrange("p a d -> p (a d)"),
                                               2.0, ps_y[:, :], ALU.mult, ALU.add).then_inc(z_ready, 1)
                wait(dve, z_ready, n + 1)
                for b in (2 * q, 2 * q + 1):
                    nc.vector.bn_stats(z_stats[:, b], z_sb[:, b]).then_inc(z_stats_ready, 1)
                for b in (2 * q, 2 * q + 1):
                    wait(dve, z_stats_ready, G4 * g + b + 1)
                    dve.sem_inc(stats_seen, 1)
                    nc.vector.bn_aggr(z_mv[:, b], z_stats[:, b]).then_inc(z_mv_ready, 1)

            def normalise(k, off, q):
                g, p = grp(k, off), off % 2
                wait(dve, z_rstd_ready, 2 * g + q + 1)
                wait(dve, stored[p], loads(k, off - 2))
                for b in (2 * q, 2 * q + 1):
                    nc.vector.tensor_scalar(out_sb[:, p, b], z_sb[:, b], z_mv[:, b, 0:1], z_rstd[:, b:b + 1],
                                            ALU.subtract, ALU.mult).then_inc(out_ready, 1)

            incidence(0, 0)
            dve.wait_ge(rows_spread, 1)
            for a in range(2):
                nc.vector.tensor_scalar(b2_half[:, a], bank[2][:, 0:d_in], 0.5, None, ALU.mult
                                        ).then_inc(set_up, 1)
            nc.vector.tensor_copy(b1_col[:, :], bank[2][:, d_in:d_in + HB]).then_inc(set_up, 1)
            dve.wait_ge(w_in, 48)
            for db in range(DB):
                nc.vector.tensor_tensor(w2_scaled[:, db], w2_rows[:, db], bank[0][:, :], ALU.mult
                                        ).then_inc(w2_prep, 1)
                nc.vector.tensor_tensor(w2_beta[:, db], w2_rows[:, db], bank[1][:, :], ALU.mult
                                        ).then_inc(w2_prep, 1)
            dve.wait_ge(w2_prep, 2 * DB)
            nc.vector.tensor_reduce(w2_sum[:, :], w2_scaled[:, :, :], AX.X, ALU.add).then_inc(w2_prep, 1)
            nc.vector.tensor_reduce(t_col[:, :], w2_beta[:, :, :], AX.X, ALU.add).then_inc(w2_prep, 1)
            dve.wait_ge(w2_prep, 2 * DB + 2)
            nc.vector.tensor_scalar(w2_mean[:, :], w2_sum[:, :], 1.0 / d_hid, None, ALU.mult).then_inc(w2_prep, 1)
            dve.wait_ge(consts, 2)
            for db in range(DB):
                nc.vector.tensor_scalar(t_wide[:, db], ones_sq[:, :], t_col[:, db:db + 1], None, ALU.mult
                                        ).then_inc(w2_prep, 1)
            dve.wait_ge(w2_prep, 3 * DB + 3)
            for db in range(DB):
                nc.vector.tensor_scalar(w2_centred[:, db], w2_scaled[:, db], w2_mean[:, db:db + 1], None,
                                        ALU.subtract).then_inc(w2_prep, 1)
            dve.wait_ge(set_hi, 1 + DB)
            for db in range(DB):
                nc.vector.tensor_tensor(w1_lo[:, db], bank[3 + db][:, :], w1_hi[:, db].bitcast(F32),
                                        ALU.subtract).then_inc(set_up, 1)
            dve.wait_ge(set_hi, 3 + DB)
            for i in range(2):
                nc.vector.tensor_tensor(w2_lo[:, 2 * i:2 * i + 2], bank[i][:, :],
                                        w2_hi[:, 2 * i:2 * i + 2].bitcast(F32), ALU.subtract).then_inc(set_up, 1)
            dve.wait_ge(t_spread, 1)
            nc.vector.tensor_copy(t_all[:, :], bank[7][:, 0:d_in]).then_inc(set_up, 1)
            dve.wait_ge(set_up, 6 + DB)

            inverses(0, 0)
            incidence(0, 1)
            u_low(0, 0)

            def iteration(k, off, first, last):
                if not first:
                    v_rows(k, off - 1, 1)
                wait(dve, v_done, G4 * grp(k, off))
                h_low(k, off, 0)
                if not first:
                    z_rows(k, off - 1, 0)
                h_low(k, off, 1)
                h_low(k, off, 2)
                if not last:
                    inverses(k, off + 1)
                h_low(k, off, 3)
                if not first:
                    z_rows(k, off - 1, 1)
                    normalise(k, off - 1, 0)
                if not (last or (off == 0 and isinstance(k, int) and k == PAIRS - 1)):
                    incidence(k, off + 2)
                h_variance(k, off, 0)
                if not first:
                    normalise(k, off - 1, 1)
                h_variance(k, off, 1)
                h_variance(k, off, 2)
                v_rows(k, off, 0)
                if not last:
                    u_low(k, off + 1)
                h_variance(k, off, 3)

            over_groups(dve, iteration)
            v_rows(PAIRS - 1, 1, 1)
            for q in range(2):
                z_rows(PAIRS - 1, 1, q)
            for q in range(2):
                normalise(PAIRS - 1, 1, q)

        @block.tensor
        def _(pe):
            def turn_incidence(k, off):
                g = grp(k, off)
                wait(pe, inc_ready, g + 1)
                wait(pe, at_ready, g)
                for j in range(G4):
                    last = nc.tensor.transpose(ps_adj[:, j * 64:(j + 1) * 64].bitcast(BF16), inc_bf[:, j],
                                               ident_bf[:, :])
                last.then_inc(inc_turned, 1)

            def sums(k, off):
                wait(pe, inc_t_ready, grp(k, off) + 1)
                for j in range(G4):
                    nc.tensor.matmul(ps_adj[:, j:j + 1], inc_bf[:, j], ones_bf[:, :], start=True, stop=True)
                for j in range(G4):
                    last = nc.tensor.matmul(ps_adj[:, G4 + j:G4 + j + 1], inc_t[:, j],
                                            edge_w[:, bass.ds(graph0(k, off) + j, 1)], start=True, stop=True)
                last.then_inc(sums_done, 1)

            def turn_scaled(k, off):
                wait(pe, scaled_ready, grp(k, off) + 1)
                for j in range(G4):
                    last = nc.tensor.transpose(ps_adj[:, j * P:(j + 1) * P], scaled[:, j], ident[:, :])
                last.then_inc(scaled_turned, 1)

            def make_at(k, off):
                wait(pe, scaled_t_ready, G4 * (grp(k, off) + 1))
                for j in range(G4):
                    last = nc.tensor.matmul(ps_adj[:, j * P:(j + 1) * P], inc_t[:, j], scaled_t[:, j],
                                            start=True, stop=True)
                last.then_inc(at_done, 1)

            def make_u(k, off):
                g, p = grp(k, off), off % 2
                wait(pe, at_ready, g + 1)
                wait(pe, x_in[p], loads(k, off))
                wait(pe, h_hi_ready, HB * g)
                for db in range(DB):
                    for j in range(G4):
                        last = nc.tensor.matmul(ps_hid[db][:, j * P:(j + 1) * P],
                                                x_sb[:, p, j, db * P:(db + 1) * P], at_sb[:, p, j],
                                                start=True, stop=True)
                    last.then_inc(u_done, 1)

            def hidden(k, off, hb):
                g = grp(k, off)
                cols = slice(hb * P, (hb + 1) * P)
                acc = ps_hid[hb % 2]
                if hb == 0:
                    wait(pe, u_lo_ready, DB * g + 1)
                    wait(pe, u_hi_ready, DB * g + DB)
                elif hb >= 2:
                    wait(pe, h_hi_ready, HB * g + hb - 1)
                terms = [(w, u_hi, db) for db in range(DB) for w in (w1_hi, w1_lo)]
                terms += [(w1_hi, u_lo, db) for db in range(DB)]
                for i, (w, u, db) in enumerate(terms):
                    if hb == 0 and i == len(terms) - 1:
                        wait(pe, u_lo_ready, DB * g + DB)
                    last = nc.tensor.matmul(acc[:, :], w[:, db, cols], u[:, db], start=(i == 0),
                                            stop=(i == len(terms) - 1))
                last.then_inc(hid_done, 1)

            def turn_h(k, off, b):
                n = G4 * grp(k, off) + b
                if b == 0:
                    wait(pe, h_hi_ready, HB * grp(k, off) + HB)
                wait(pe, h_stats_ready, n - 1)
                for hb in range(HB):
                    last = nc.tensor.transpose(ps_ht[b % 2][:, hb * P:(hb + 1) * P],
                                               h_sb[:, hb, b * P:(b + 1) * P], ident[:, :])
                last.then_inc(ht_done, 1)

            def second(k, off, b):
                g = grp(k, off)
                nodes_b = slice(b * P, (b + 1) * P)
                acc = ps_v[b // 2][:, (b % 2) * d_in:(b % 2 + 1) * d_in]
                if b % 2 == 0:
                    wait(pe, v_ready, G4 * (g - 1) + b + 2)
                for hb in range(HB):
                    if b == 0:
                        wait(pe, h_lo_ready, HB * g + hb + 1)
                    terms = [(h_hi, w2_hi), (h_hi, w2_lo), (h_lo, w2_hi)]
                    for i, (h, w) in enumerate(terms):
                        last = nc.tensor.matmul(acc, h[:, hb, nodes_b], w[:, hb], start=(hb == 0 and i == 0),
                                                stop=(hb == HB - 1 and i == 2))
                last.then_inc(v_done, 1)

            def mix(k, off, q):
                g, p = grp(k, off), off % 2
                wait(pe, v_ready, G4 * g + 2 * q + 2)
                wait(pe, z_ready, 2 * g + q)
                for b in (2 * q, 2 * q + 1):
                    last = nc.tensor.matmul(ps_y[:, (b % 2) * d_in:(b % 2 + 1) * d_in], at_sb[:, p, b], v_sb[:, b],
                                            start=True, stop=True)
                last.then_inc(y_done, 1)

            pe.wait_ge(rows_in, 64)
            pe.wait_ge(consts, 2)
            nc.tensor.matmul(bank[0][:, :], ones_row[:, :], gamma_row[:, :], start=True, stop=True)
            nc.tensor.matmul(bank[1][:, :], ones_row[:, :], beta_row[:, :], start=True, stop=True)
            for hb in range(HB):
                nc.tensor.matmul(bank[2][:, d_in + hb:d_in + hb + 1], b1_row[:, hb * P:(hb + 1) * P],
                                 ones_row[:, 0:1], start=True, stop=True)
            nc.tensor.matmul(bank[2][:, 0:d_in], ones_row[:, :], b2_row[:, :], start=True, stop=True
                             ).then_inc(rows_spread, 1)
            pe.wait_ge(w_in, 48)
            nc.tensor.transpose(bank[5][:, 0:graphs], first_rows[:, :], ident[:, :]).then_inc(edge_turned, 1)
            for db in range(DB):
                for hb in range(HB):
                    last = nc.tensor.transpose(bank[3 + db][:, hb * P:(hb + 1) * P],
                                               w1_rows[:, hb, db * P:(db + 1) * P], ident[:, :])
            last.then_inc(w1_turned, 1)
            pe.wait_ge(w2_prep, 4 * DB + 3)
            for hb in range(HB):
                for db in range(DB):
                    last = nc.tensor.transpose(bank[hb // 2][:, (hb % 2) * d_in + db * P:(hb % 2) * d_in + (db + 1) * P],
                                               w2_centred[:, db, hb * P:(hb + 1) * P], ident[:, :])
            last.then_inc(w2_turned, 1)
            for db in range(DB):
                last = nc.tensor.matmul(bank[7][:, db * P:(db + 1) * P], t_wide[:, db], ident[:, :],
                                        start=True, stop=True)
            last.then_inc(t_spread, 1)

            turn_incidence(0, 0)
            pe.wait_ge(set_hi, 1)
            sums(0, 0)
            turn_scaled(0, 0)
            make_at(0, 0)
            pe.wait_ge(set_up, 6 + DB)
            make_u(0, 0)

            def iteration(k, off, first, last):
                hidden(k, off, 0)
                hidden(k, off, 1)
                if not first:
                    mix(k, off - 1, 0)
                hidden(k, off, 2)
                if not last:
                    turn_incidence(k, off + 1)
                hidden(k, off, 3)
                if not last:
                    sums(k, off + 1)
                if not first:
                    mix(k, off - 1, 1)
                turn_h(k, off, 0)
                second(k, off, 0)
                if not last:
                    turn_scaled(k, off + 1)
                turn_h(k, off, 1)
                second(k, off, 1)
                if not last:
                    make_at(k, off + 1)
                turn_h(k, off, 2)
                second(k, off, 2)
                if not last:
                    make_u(k, off + 1)
                turn_h(k, off, 3)
                second(k, off, 3)

            over_groups(pe, iteration)
            mix(PAIRS - 1, 1, 0)
            mix(PAIRS - 1, 1, 1)


_INS = ["x", "adj", "L0_gnn_W1", "L0_gnn_b1", "L0_gnn_gamma", "L0_gnn_beta", "L0_gnn_W2", "L0_gnn_b2"]


def kernel(**inputs):
    import numpy as np
    import concourse.bacc as bacc
    from concourse.bass_utils import run_bass_kernel_spmd as run

    nc = bacc.Bacc("TRN2", target_bir_lowering=False, num_devices=1)
    arrays, args = {}, []
    for name in _INS:
        a = np.ascontiguousarray(inputs[name])
        arrays[f"in_{name}"] = a
        args.append(nc.dram_tensor(f"in_{name}", a.shape, mybir.dt.from_np(a.dtype), kind="ExternalInput").ap())
    out = nc.dram_tensor("out", arrays["in_x"].shape, F32, kind="ExternalOutput").ap()
    hypergraph_block(nc, *args, out)
    r = run(nc, [arrays], core_ids=[0])
    return r.results[0]["out"]
```

```python
import concourse.bass as bass
from concourse import mybir
from contextlib import ExitStack

F32 = mybir.dt.float32
F32R = mybir.dt.float32r
BF16 = mybir.dt.bfloat16
ALU = mybir.AluOpType
ACT = mybir.ActivationFunctionType
AX = mybir.AxisListType

P = 128
LN_EPS = 1e-5
TINY = 1.1754944e-38


def hypergraph_block(nc, x, adj, w1, b1, gamma, beta, w2, b2, out):
    graphs, nodes, d_in = x.shape
    d_hid = w1.shape[0]
    assert nodes == P and d_in == w2.shape[0]
    DB = d_in // P
    HB = d_hid // P
    G4 = 512 // P
    GROUPS = graphs // G4
    PAIRS = GROUPS // 2

    ctx = ExitStack()
    with ctx:
        def sb(name, shape, dt=F32):
            return ctx.enter_context(nc.sbuf_tensor(name, shape, dt))

        def sem(name):
            return ctx.enter_context(nc.semaphore(name))

        ident = sb("ident", [P, P])
        ident_bf = sb("ident_bf", [P, P], BF16)
        ones_sq = sb("ones_sq", [P, P])
        ones_bf = sb("ones_bf", [P, 1], BF16)
        minus_half = sb("minus_half", [P, 2])
        eps = sb("eps", [P, 2])
        zeros = sb("zeros", [P, 2])
        w1_rows = sb("w1_rows", [P, HB, d_in])
        w2_rows = sb("w2_rows", [P, DB, d_hid])
        w2_scaled = sb("w2_scaled", [P, DB, d_hid])
        w2_centred = sb("w2_centred", [P, DB, d_hid])
        w2_beta = sb("w2_beta", [P, DB, d_hid])
        gamma_all = sb("gamma_all", [P, d_hid])
        beta_all = sb("beta_all", [P, d_hid])
        b2_all = sb("b2_all", [P, d_in])
        b1_rows = sb("b1_rows", [HB, P])
        first_rows = sb("first_rows", [P, P])
        w2_sum = sb("w2_sum", [P, DB])
        w2_mean = sb("w2_mean", [P, DB])
        t_col = sb("t_col", [P, DB])
        t_wide = sb("t_wide", [P, DB, P])
        b1_col = sb("b1_col", [P, HB])
        b2_half = sb("b2_half", [P, 2, d_in])
        t_all = sb("t_all", [P, d_in])
        edge_w = sb("edge_w", [P, graphs])
        edge_rest = sb("edge_rest", [P, 2, graphs])
        edge_parts = sb("edge_parts", [P, 3 * graphs], BF16)
        w1_hi = sb("w1_hi", [P, DB, d_hid], F32R)
        w1_lo = sb("w1_lo", [P, DB, d_hid], F32R)
        w2_hi = sb("w2_hi", [P, HB, d_in], F32R)
        w2_lo = sb("w2_lo", [P, HB, d_in], F32R)

        adj_sb = sb("adj_sb", [P, 2, G4, P])
        x_sb = sb("x_sb", [P, 2, G4, d_in])
        xb_sb = sb("xb_sb", [P, 2, G4, d_in])
        at_hi = sb("at_hi", [P, 2, G4, P], F32R)
        at_lo = sb("at_lo", [P, 2, G4, P], F32R)
        out_sb = sb("out_sb", [P, 2, G4, d_in])
        inc_bf = sb("inc_bf", [P, G4, P], BF16)
        inc_t = sb("inc_t", [P, G4, P])
        inc_t_bf = sb("inc_t_bf", [P, G4, P], BF16)
        group_w = sb("group_w", [P, 3 * G4], BF16)
        d_sum = sb("d_sum", [P, G4])
        safe = sb("safe", [P, 2 * G4])
        inv = sb("inv", [P, 2 * G4])
        d_pos = sb("d_pos", [P, G4])
        d_inv = sb("d_inv", [P, G4])
        scaled = sb("scaled", [P, G4, P])
        scaled_t = sb("scaled_t", [P, G4, P])
        u_hi = sb("u_hi", [P, DB, G4 * P], F32R)
        u_lo = sb("u_lo", [P, DB, G4 * P], F32R)
        h_sb = sb("h_sb", [P, HB, G4 * P])
        h_hi = sb("h_hi", [P, HB, G4 * P], F32R)
        h_lo = sb("h_lo", [P, HB, G4 * P], F32R)
        at_sb = sb("at_sb", [P, G4, P])
        v_sb = sb("v_sb", [P, G4, d_in])
        v_hi = sb("v_hi", [P, G4, d_in], F32R)
        v_lo = sb("v_lo", [P, G4, d_in], F32R)
        z_sb = sb("z_sb", [P, G4, d_in])
        h_stats = sb("h_stats", [P, G4, 6])
        h_mv = sb("h_mv", [P, G4, 2])
        h_var = sb("h_var", [P, G4])
        h_rstd = sb("h_rstd", [P, G4])
        z_stats = sb("z_stats", [P, G4, 6])
        z_mv = sb("z_mv", [P, G4, 2])
        z_var = sb("z_var", [P, G4])
        z_rstd = sb("z_rstd", [P, G4])
        z_scaled_mean = sb("z_scaled_mean", [P, G4])
        z_shift = sb("z_shift", [P, G4])

        bank = [ctx.enter_context(nc.psum_tensor(f"bank{i}", [P, 512], F32)) for i in range(8)]
        ps_hid = bank[0:2]
        ps_v = bank[2:4]
        ps_ht = bank[4:6]
        ps_adj = bank[6]
        ps_y = bank[7]

        ps_rows = bank[5]
        ps_w = bank[3:5]

        first_rows_in = sem("first_rows_in")
        w1_in = sem("w1_in")
        w2_in = sem("w2_in")
        gamma_in = sem("gamma_in")
        beta_in = sem("beta_in")
        b1_in = sem("b1_in")
        b2_in = sem("b2_in")
        adj_in = [sem(f"adj_in{p}") for p in range(2)]
        x_in = [sem(f"x_in{p}") for p in range(2)]
        stored = [sem(f"stored{p}") for p in range(2)]
        zeroed = sem("zeroed")
        consts = sem("consts")
        edge_turned = sem("edge_turned")
        edge_split = sem("edge_split")
        w1_turned = sem("w1_turned")
        w1_hi_ready = sem("w1_hi_ready")
        w1_lo_ready = sem("w1_lo_ready")
        b2_ready = sem("b2_ready")
        b1_turned = sem("b1_turned")
        b1_ready = sem("b1_ready")
        w2_scaling = sem("w2_scaling")
        w2_centring = sem("w2_centring")
        w2_turned = sem("w2_turned")
        w2_hi_ready = sem("w2_hi_ready")
        w2_lo_ready = sem("w2_lo_ready")
        t_prep = sem("t_prep")
        t_spread = sem("t_spread")
        t_ready = sem("t_ready")
        inc_turned = sem("inc_turned")
        sums_done = sem("sums_done")
        scaled_turned = sem("scaled_turned")
        at_done = sem("at_done")
        u_done = sem("u_done")
        hid_done = sem("hid_done")
        ht_done = sem("ht_done")
        v_done = sem("v_done")
        y_done = sem("y_done")
        inc_t_ready = sem("inc_t_ready")
        scaled_t_ready = sem("scaled_t_ready")
        at_ready = sem("at_ready")
        at_hi_ready = sem("at_hi_ready")
        v_hi_ready = sem("v_hi_ready")
        u_hi_ready = sem("u_hi_ready")
        h_ready = sem("h_ready")
        h_hi_ready = sem("h_hi_ready")
        inc_ready = sem("inc_ready")
        d_summed = sem("d_summed")
        sums_safe = sem("sums_safe")
        inv_ready = sem("inv_ready")
        d_inv_ready = sem("d_inv_ready")
        scaled_ready = sem("scaled_ready")
        u_lo_ready = sem("u_lo_ready")
        h_lo_ready = sem("h_lo_ready")
        h_stats_ready = sem("h_stats_ready")
        stats_seen = sem("stats_seen")
        h_mv_ready = sem("h_mv_ready")
        v_ready = sem("v_ready")
        z_ready = sem("z_ready")
        z_stats_ready = sem("z_stats_ready")
        z_mv_ready = sem("z_mv_ready")
        out_ready = sem("out_ready")
        group_w_ready = sem("group_w_ready")
        xb_ready = sem("xb_ready")
        at_lo_ready = sem("at_lo_ready")
        v_lo_ready = sem("v_lo_ready")
        h_eps = sem("h_eps")
        h_rstd_ready = sem("h_rstd_ready")
        z_eps = sem("z_eps")
        z_rstd_ready = sem("z_rstd_ready")
        z_mean_scaled = sem("z_mean_scaled")
        z_shift_ready = sem("z_shift_ready")

        adj_dram = adj.rearrange("n i e -> i n e")
        x_dram = x.rearrange("n c d -> c n d")
        out_dram = out.rearrange("n c d -> c n d")

        def wait(eng, s, value):
            if not isinstance(value, int) or value > 0:
                eng.wait_ge(s, value)

        def grp(k, off):
            return 2 * k + off

        def graph0(k, off):
            return 2 * G4 * k + G4 * off

        def loads(k, off):
            return 16 * k + 16 * (off // 2 + 1)

        def before_last(k, off):
            return isinstance(k, int) and k == PAIRS - 1 and off == 0

        def over_groups(eng, iteration):
            iteration(0, 0, True, False)
            iteration(0, 1, False, False)
            with eng.Fori(1, PAIRS - 1) as k:
                for off in range(2):
                    iteration(k, off, False, False)
            iteration(PAIRS - 1, 0, False, False)
            iteration(PAIRS - 1, 1, False, True)

        block = ctx.enter_context(nc.Block())

        @block.sync
        def _(sp):
            def load_adj(k, off):
                sp.dma_start(adj_sb[:, off % 2], adj_dram[:, bass.ds(graph0(k, off), G4)]
                             ).then_inc(adj_in[off % 2], 16)

            def load_x(k, off):
                sp.dma_start(x_sb[:, off % 2], x_dram[:, bass.ds(graph0(k, off), G4)]
                             ).then_inc(x_in[off % 2], 16)

            def store(k, off):
                wait(sp, out_ready, G4 * (grp(k, off) + 1))
                sp.dma_start(out_dram[:, bass.ds(graph0(k, off), G4)], out_sb[:, off % 2]
                             ).then_inc(stored[off % 2], 16)

            load_adj(0, 0)
            sp.dma_start(first_rows[:, :], adj[:, 0, :]).then_inc(first_rows_in, 16)
            sp.dma_start(w1_rows[:, :, :], w1.rearrange("(b p) d -> p b d", p=P)).then_inc(w1_in, 16)
            load_x(0, 0)
            sp.dma_start(b1_rows[:, :], b1.rearrange("(b p) -> b p", p=P)).then_inc(b1_in, 16)
            sp.dma_start(w2_rows[:, :, :], w2.rearrange("(b p) h -> p b h", p=P)).then_inc(w2_in, 16)
            for row, values, arrived in ((gamma_all, gamma, gamma_in), (beta_all, beta, beta_in),
                                         (b2_all, b2, b2_in)):
                sp.dma_start(row[:, :], values.partition_broadcast(P)).then_inc(arrived, 16)
            load_adj(0, 1)
            load_x(0, 1)

            def iteration(k, off, first, last):
                g = grp(k, off)
                if not (last or before_last(k, off)):
                    wait(sp, inc_ready, g + 1)
                    load_adj(k, off + 2)
                if not (isinstance(k, int) and k == 0):
                    store(k, off - 2)
                if not (last or before_last(k, off)):
                    wait(sp, u_done, DB * (g + 1))
                    wait(sp, xb_ready, 2 * (g + 1))
                    load_x(k, off + 2)

            over_groups(sp, iteration)
            store(PAIRS - 1, 0)
            p, n0 = 1, graphs - G4
            for q in range(2):
                sp.wait_ge(out_ready, n0 + 2 * q + 2)
                sp.dma_start(out_dram[:, n0 + 2 * q:n0 + 2 * q + 2], out_sb[:, p, 2 * q:2 * q + 2]
                             ).then_inc(stored[p], 16)
            sp.wait_ge(stored[0], 16 * PAIRS)
            sp.wait_ge(stored[1], 16 * PAIRS + 16)

        @block.gpsimd
        def _(pool):
            nc.gpsimd.memset(ident[:, :], 0.0).then_inc(zeroed, 1)
            nc.gpsimd.memset(ident_bf[:, :], 0.0).then_inc(zeroed, 1)
            nc.gpsimd.memset(ones_sq[:, :], 1.0)
            nc.gpsimd.memset(ones_bf[:, :], 1.0)
            nc.gpsimd.memset(minus_half[:, :], -0.5)
            nc.gpsimd.memset(eps[:, :], LN_EPS)
            nc.gpsimd.memset(zeros[:, :], 0.0)
            pool.wait_ge(zeroed, 2)
            for m in (ident, ident_bf):
                nc.gpsimd.affine_select(out=m[:, :], in_=m[:, :], compare_op=ALU.not_equal, fill=1.0,
                                        base=0, pattern=[[-1, P]], channel_multiplier=1).then_inc(consts, 1)

            def residual(k, off, q):
                g, p = grp(k, off), off % 2
                wait(pool, x_in[p], loads(k, off))
                wait(pool, z_ready, 2 * (g - 2) + q + 1)
                nc.gpsimd.tensor_tensor(xb_sb[:, p, 2 * q:2 * q + 2], x_sb[:, p, 2 * q:2 * q + 2],
                                        b2_half[:, :, :], ALU.add).then_inc(xb_ready, 1)

            def edge_columns(k, off):
                g = grp(k, off)
                wait(pool, sums_done, g)
                nc.gpsimd.tensor_copy(group_w[:, :], edge_parts[:, bass.ds(3 * graph0(k, off), 3 * G4)]
                                      ).then_inc(group_w_ready, 1)

            def rstd(k, off, q, mv, mv_ready, var, eps_done, r, r_ready):
                n = 2 * grp(k, off) + q
                cols = slice(2 * q, 2 * q + 2)
                wait(pool, mv_ready, 2 * n + 2)
                nc.gpsimd.tensor_tensor(var[:, cols], mv[:, cols, 1], eps[:, :], ALU.add
                                        ).then_inc(eps_done, 1)
                wait(pool, eps_done, n + 1)
                nc.gpsimd.tensor_tensor(r[:, cols], var[:, cols], minus_half[:, :], ALU.pow
                                        ).then_inc(r_ready, 1)

            def low_at(k, off):
                g, p = grp(k, off), off % 2
                wait(pool, at_hi_ready, g + 1)
                wait(pool, y_done, 2 * (g - 1))
                nc.gpsimd.tensor_tensor(at_lo[:, p], at_sb[:, :], at_hi[:, p].bitcast(F32), ALU.subtract
                                        ).then_inc(at_lo_ready, 1)

            def low_v(k, off, q):
                g, n = grp(k, off), 2 * grp(k, off) + q
                rows = slice(2 * q, 2 * q + 2)
                wait(pool, v_hi_ready, n + 1)
                wait(pool, y_done, 2 * (g - 1) + q + 1)
                nc.gpsimd.tensor_tensor(v_lo[:, rows], v_sb[:, rows], v_hi[:, rows].bitcast(F32), ALU.subtract
                                        ).then_inc(v_lo_ready, 1)

            def h_scale(k, off, q):
                wait(pool, v_ready, G4 * (grp(k, off) - 1) + 2 * q + 2)
                rstd(k, off, q, h_mv, h_mv_ready, h_var, h_eps, h_rstd, h_rstd_ready)

            def z_scale(k, off, q):
                wait(pool, out_ready, G4 * (grp(k, off) - 1) + 2 * q + 2)
                rstd(k, off, q, z_mv, z_mv_ready, z_var, z_eps, z_rstd, z_rstd_ready)
                if isinstance(k, int) and grp(k, off) == GROUPS - 1:
                    return
                n, cols = 2 * grp(k, off) + q, slice(2 * q, 2 * q + 2)
                wait(pool, z_rstd_ready, n + 1)
                nc.gpsimd.tensor_tensor(z_scaled_mean[:, cols], z_mv[:, cols, 0], z_rstd[:, cols], ALU.mult
                                        ).then_inc(z_mean_scaled, 1)
                wait(pool, z_mean_scaled, n + 1)
                nc.gpsimd.tensor_tensor(z_shift[:, cols], zeros[:, :], z_scaled_mean[:, cols], ALU.subtract
                                        ).then_inc(z_shift_ready, 1)

            pool.wait_ge(edge_split, 6)
            edge_columns(0, 0)
            edge_columns(0, 1)
            for row, arrived, product, done in ((gamma_all, gamma_in, w2_scaled, w2_scaling),
                                                (beta_all, beta_in, w2_beta, t_prep)):
                pool.wait_ge(w2_in, 16)
                pool.wait_ge(arrived, 16)
                for db in range(DB):
                    nc.gpsimd.tensor_tensor(product[:, db], w2_rows[:, db], row[:, :], ALU.mult
                                            ).then_inc(done, 1)
            low_at(0, 0)
            pool.wait_ge(b2_ready, 2)

            def iteration(k, off, first, last):
                if not first:
                    h_scale(k, off - 1, 1)
                residual(k, off, 0)
                residual(k, off, 1)
                if not first:
                    low_v(k, off - 1, 1)
                    z_scale(k, off - 1, 0)
                if not last:
                    if not before_last(k, off):
                        edge_columns(k, off + 2)
                    low_at(k, off + 1)
                h_scale(k, off, 0)
                if not first:
                    z_scale(k, off - 1, 1)
                if not last:
                    low_v(k, off, 0)

            over_groups(pool, iteration)
            h_scale(PAIRS - 1, 1, 1)
            z_scale(PAIRS - 1, 1, 0)
            z_scale(PAIRS - 1, 1, 1)

        @block.scalar
        def _(act):
            def h_block(k, off, hb):
                g = grp(k, off)
                wait(act, hid_done, HB * g + hb + 1)
                if hb == 0:
                    wait(act, v_done, G4 * g)
                    wait(act, ht_done, G4 * g)
                    wait(act, h_lo_ready, HB * g)
                nc.scalar.activation(h_sb[:, hb], ps_hid[hb % 2][:, :], ACT.Relu, bias=b1_col[:, hb:hb + 1]
                                     ).then_inc(h_ready, 1)
                nc.scalar.activation(h_hi[:, hb], ps_hid[hb % 2][:, :], ACT.Relu, bias=b1_col[:, hb:hb + 1]
                                     ).then_inc(h_hi_ready, 1)

            def copy_inc_t(k, off):
                g = grp(k, off)
                wait(act, inc_turned, g + 1)
                wait(act, at_done, g)
                nc.scalar.activation(inc_t_bf[:, :, :], ps_adj[:, 0:256].bitcast(BF16), ACT.Copy)
                nc.scalar.activation(inc_t[:, :, :], ps_adj[:, 0:256].bitcast(BF16), ACT.Copy
                                     ).then_inc(inc_t_ready, 1)

            def copy_at(k, off):
                g = grp(k, off)
                wait(act, at_done, g + 1)
                wait(act, u_done, DB * g)
                wait(act, at_lo_ready, g)
                nc.scalar.activation(at_sb[:, :, :], ps_adj[:, :], ACT.Copy).then_inc(at_ready, 1)
                wait(act, y_done, 2 * (g - 1))
                nc.scalar.activation(at_hi[:, off % 2], ps_adj[:, :], ACT.Copy).then_inc(at_hi_ready, 1)

            def v_high(k, off, q):
                g, rows = grp(k, off), slice(2 * q, 2 * q + 2)
                wait(act, v_ready, G4 * g + 2 * q + 2)
                wait(act, y_done, 2 * (g - 1) + q + 1)
                nc.scalar.activation(v_hi[:, rows], v_sb[:, rows], ACT.Copy).then_inc(v_hi_ready, 1)

            def u_high(k, off):
                g = grp(k, off)
                wait(act, hid_done, HB * g)
                for db in range(DB):
                    wait(act, u_done, DB * g + db + 1)
                    nc.scalar.activation(u_hi[:, db], ps_hid[db][:, :], ACT.Copy).then_inc(u_hi_ready, 1)

            def normalise(k, off, q):
                g, p = grp(k, off), off % 2
                wait(act, z_shift_ready, 2 * g + q + 1)
                wait(act, stored[p], loads(k, off - 2))
                for b in (2 * q, 2 * q + 1):
                    nc.scalar.activation(out_sb[:, p, b], z_sb[:, b], ACT.Identity, scale=z_rstd[:, b:b + 1],
                                         bias=z_shift[:, b:b + 1]).then_inc(out_ready, 1)

            act.wait_ge(edge_turned, 1)
            nc.scalar.activation(edge_w[:, :], ps_rows[:, 0:graphs], ACT.Copy).then_inc(edge_split, 1)
            copy_inc_t(0, 0)
            act.wait_ge(w1_turned, 1)
            for db in range(DB):
                nc.scalar.activation(w1_hi[:, db], ps_w[db][:, :], ACT.Copy).then_inc(w1_hi_ready, 1)
            act.wait_ge(b2_in, 16)
            for a in range(2):
                nc.scalar.activation(b2_half[:, a], b2_all[:, :], ACT.Copy, scale=0.5).then_inc(b2_ready, 1)
            copy_at(0, 0)
            u_high(0, 0)
            act.wait_ge(w2_turned, 1)
            for i in range(2):
                nc.scalar.activation(w2_hi[:, 2 * i:2 * i + 2], ps_w[i][:, :], ACT.Copy).then_inc(w2_hi_ready, 1)
            copy_inc_t(0, 1)
            act.wait_ge(b1_ready, 1)

            def iteration(k, off, first, last):
                h_block(k, off, 0)
                if not (isinstance(k, int) and k == 0):
                    normalise(k, off - 2, 1)
                h_block(k, off, 1)
                if not first:
                    v_high(k, off - 1, 1)
                h_block(k, off, 2)
                h_block(k, off, 3)
                if not last:
                    copy_at(k, off + 1)
                    u_high(k, off + 1)
                if not first:
                    normalise(k, off - 1, 0)
                if not (last or before_last(k, off)):
                    copy_inc_t(k, off + 2)
                v_high(k, off, 0)

            over_groups(act, iteration)
            normalise(PAIRS - 1, 0, 1)
            v_high(PAIRS - 1, 1, 1)

        @block.vector
        def _(dve):
            def incidence(k, off):
                g, p = grp(k, off), off % 2
                wait(dve, adj_in[p], loads(k, off))
                wait(dve, inc_turned, g)
                wait(dve, scaled_ready, g)
                nc.vector.tensor_scalar(inc_bf[:, :, :], adj_sb[:, p], 0.0, None, ALU.not_equal
                                        ).then_inc(inc_ready, 1)

            def inverses(k, off):
                g = grp(k, off)
                wait(dve, sums_done, g + 1)
                wait(dve, scaled_t_ready, g)
                wait(dve, scaled_ready, g)
                nc.vector.tensor_scalar(safe[:, 0:G4], ps_adj[:, 0:G4], 1.0, None, ALU.max).then_inc(sums_safe, 1)
                nc.vector.tensor_reduce(d_sum[:, :], ps_adj[:, G4:G4 + 3 * G4].rearrange("p (j w) -> p j w", w=3),
                                        AX.X, ALU.add).then_inc(d_summed, 1)
                wait(dve, d_summed, g + 1)
                nc.vector.tensor_scalar(safe[:, G4:2 * G4], d_sum[:, :], TINY, None, ALU.max
                                        ).then_inc(sums_safe, 1)
                nc.vector.tensor_scalar(d_pos[:, :], d_sum[:, :], 0.0, None, ALU.is_gt
                                        ).then_inc(sums_safe, 1)
                wait(dve, sums_safe, 3 * g + 3)
                nc.vector.reciprocal(inv[:, :], safe[:, :]).then_inc(inv_ready, 1)
                wait(dve, inv_ready, g + 1)
                nc.vector.tensor_tensor(d_inv[:, :], inv[:, G4:2 * G4], d_pos[:, :], ALU.mult
                                        ).then_inc(d_inv_ready, 1)

            def scale(k, off):
                g = grp(k, off)
                wait(dve, d_inv_ready, g + 1)
                wait(dve, scaled_turned, g)
                for j in range(G4):
                    last = nc.vector.tensor_scalar(scaled[:, j], inc_bf[:, j], d_inv[:, j:j + 1], None, ALU.mult)
                last.then_inc(scaled_ready, 1)

            def scale_t(k, off):
                g = grp(k, off)
                wait(dve, scaled_turned, g + 1)
                wait(dve, at_done, g)
                nc.vector.tensor_tensor(scaled_t[:, :, :], ps_adj[:, :].rearrange("p (j i) -> p j i", i=P),
                                        inv[:, 0:G4].unsqueeze(2).broadcast_to([P, G4, P]), ALU.mult
                                        ).then_inc(scaled_t_ready, 1)

            def u_low(k, off, db):
                wait(dve, u_hi_ready, DB * grp(k, off) + db + 1)
                nc.vector.tensor_tensor(u_lo[:, db], ps_hid[db][:, :], u_hi[:, db].bitcast(F32),
                                        ALU.subtract).then_inc(u_lo_ready, 1)

            def h_low(k, off, hb):
                g = grp(k, off)
                wait(dve, h_ready, HB * g + hb + 1)
                wait(dve, h_hi_ready, HB * g + hb + 1)
                nc.vector.tensor_tensor(h_lo[:, hb], h_sb[:, hb], h_hi[:, hb].bitcast(F32),
                                        ALU.subtract).then_inc(h_lo_ready, 1)

            def h_variance(k, off, b):
                n = G4 * grp(k, off) + b
                wait(dve, ht_done, n + 1)
                wait(dve, h_rstd_ready, 2 * (grp(k, off) - 1) + b // 2 + 1)
                nc.vector.bn_stats(h_stats[:, b], ps_ht[b % 2][:, :]).then_inc(h_stats_ready, 1)
                wait(dve, h_stats_ready, n + 1)
                dve.sem_inc(stats_seen, 1)
                nc.vector.bn_aggr(h_mv[:, b], h_stats[:, b]).then_inc(h_mv_ready, 1)

            def v_rows(k, off, q):
                g = grp(k, off)
                wait(dve, h_rstd_ready, 2 * g + q + 1)
                wait(dve, v_done, G4 * g + 2 * q + 2)
                wait(dve, v_lo_ready, 2 * (g - 1) + q + 1)
                for b in (2 * q, 2 * q + 1):
                    nc.vector.scalar_tensor_tensor(v_sb[:, b], ps_v[q][:, (b % 2) * d_in:(b % 2 + 1) * d_in],
                                                   h_rstd[:, b:b + 1], t_all[:, :], ALU.mult, ALU.add
                                                   ).then_inc(v_ready, 1)

            def z_rows(k, off, q):
                g, p, n = grp(k, off), off % 2, 2 * grp(k, off) + q
                wait(dve, y_done, n + 1)
                wait(dve, xb_ready, n + 1)
                wait(dve, out_ready, G4 * (g - 1) + 2 * q + 2)
                nc.vector.scalar_tensor_tensor(z_sb[:, 2 * q:2 * q + 2].rearrange("p a d -> p (a d)"),
                                               xb_sb[:, p, 2 * q:2 * q + 2].rearrange("p a d -> p (a d)"),
                                               2.0, ps_y[:, :], ALU.mult, ALU.add).then_inc(z_ready, 1)

            def z_moments(k, off, q):
                g, n = grp(k, off), 2 * grp(k, off) + q
                wait(dve, z_ready, n + 1)
                wait(dve, z_rstd_ready, 2 * (g - 1) + q + 1)
                for b in (2 * q, 2 * q + 1):
                    nc.vector.bn_stats(z_stats[:, b], z_sb[:, b]).then_inc(z_stats_ready, 1)
                for b in (2 * q, 2 * q + 1):
                    wait(dve, z_stats_ready, G4 * g + b + 1)
                    dve.sem_inc(stats_seen, 1)
                    nc.vector.bn_aggr(z_mv[:, b], z_stats[:, b]).then_inc(z_mv_ready, 1)

            incidence(0, 0)
            dve.wait_ge(edge_split, 1)
            parts = edge_parts[:, :].rearrange("p (n w) -> p w n", w=3)
            rest = edge_w[:, :]
            for i in range(3):
                nc.vector.tensor_copy(parts[:, i], rest).then_inc(edge_split, 1)
                if i < 2:
                    dve.wait_ge(edge_split, 2 * i + 2)
                    nc.vector.tensor_tensor(edge_rest[:, i], rest, parts[:, i], ALU.subtract).then_inc(edge_split, 1)
                    dve.wait_ge(edge_split, 2 * i + 3)
                    rest = edge_rest[:, i]
            inverses(0, 0)
            scale(0, 0)
            incidence(0, 1)
            scale_t(0, 0)
            dve.wait_ge(w2_scaling, DB)
            nc.vector.tensor_reduce(w2_sum[:, :], w2_scaled[:, :, :], AX.X, ALU.add).then_inc(w2_centring, 1)
            dve.wait_ge(w1_hi_ready, DB)
            for db in range(DB):
                nc.vector.tensor_tensor(w1_lo[:, db], ps_w[db][:, :], w1_hi[:, db].bitcast(F32),
                                        ALU.subtract).then_inc(w1_lo_ready, 1)
            dve.wait_ge(b1_turned, 1)
            nc.vector.tensor_copy(b1_col[:, :], ps_rows[:, graphs:graphs + HB]).then_inc(b1_ready, 1)
            dve.wait_ge(w2_centring, 1)
            nc.vector.tensor_scalar(w2_mean[:, :], w2_sum[:, :], 1.0 / d_hid, None, ALU.mult
                                    ).then_inc(w2_centring, 1)
            dve.wait_ge(w2_centring, 2)
            for db in range(DB):
                nc.vector.tensor_scalar(w2_centred[:, db], w2_scaled[:, db], w2_mean[:, db:db + 1], None,
                                        ALU.subtract).then_inc(w2_centring, 1)
            dve.wait_ge(t_prep, DB)
            nc.vector.tensor_reduce(t_col[:, :], w2_beta[:, :, :], AX.X, ALU.add).then_inc(t_prep, 1)
            dve.wait_ge(t_prep, DB + 1)
            for db in range(DB):
                nc.vector.tensor_scalar(t_wide[:, db], ones_sq[:, :], t_col[:, db:db + 1], None, ALU.mult
                                        ).then_inc(t_prep, 1)
            for db in range(DB):
                u_low(0, 0, db)
            dve.wait_ge(w2_hi_ready, 2)
            for i in range(2):
                nc.vector.tensor_tensor(w2_lo[:, 2 * i:2 * i + 2], ps_w[i][:, :],
                                        w2_hi[:, 2 * i:2 * i + 2].bitcast(F32), ALU.subtract
                                        ).then_inc(w2_lo_ready, 1)
            dve.wait_ge(t_spread, 1)
            nc.vector.tensor_copy(t_all[:, :], ps_rows[:, 0:d_in]).then_inc(t_ready, 1)
            dve.wait_ge(t_ready, 1)

            def low_v_last(q):
                rows = slice(2 * q, 2 * q + 2)
                dve.wait_ge(v_hi_ready, 2 * (GROUPS - 1) + q + 1)
                dve.wait_ge(y_done, 2 * (GROUPS - 2) + q + 1)
                nc.vector.tensor_tensor(v_lo[:, rows], v_sb[:, rows], v_hi[:, rows].bitcast(F32), ALU.subtract
                                        ).then_inc(v_lo_ready, 1)

            def normalise_last(q):
                dve.wait_ge(z_rstd_ready, 2 * (GROUPS - 1) + q + 1)
                dve.wait_ge(stored[1], 16 * (PAIRS - 1))
                for b in (2 * q, 2 * q + 1):
                    nc.vector.tensor_scalar(out_sb[:, 1, b], z_sb[:, b], z_mv[:, b, 0:1], z_rstd[:, b:b + 1],
                                            ALU.subtract, ALU.mult).then_inc(out_ready, 1)

            def iteration(k, off, first, last):
                if not last:
                    inverses(k, off + 1)
                    scale(k, off + 1)
                if not first:
                    v_rows(k, off - 1, 1)
                wait(dve, v_done, G4 * grp(k, off))
                h_low(k, off, 0)
                if not (last or before_last(k, off)):
                    incidence(k, off + 2)
                h_low(k, off, 1)
                if not last:
                    scale_t(k, off + 1)
                h_low(k, off, 2)
                if not first:
                    z_rows(k, off - 1, 0)
                h_low(k, off, 3)
                if not first:
                    z_moments(k, off - 1, 0)
                h_variance(k, off, 0)
                if not first:
                    z_rows(k, off - 1, 1)
                if not last:
                    u_low(k, off + 1, 0)
                h_variance(k, off, 1)
                if not last:
                    u_low(k, off + 1, 1)
                if not first:
                    z_moments(k, off - 1, 1)
                h_variance(k, off, 2)
                v_rows(k, off, 0)
                h_variance(k, off, 3)

            over_groups(dve, iteration)
            low_v_last(0)
            v_rows(PAIRS - 1, 1, 1)
            z_rows(PAIRS - 1, 1, 0)
            low_v_last(1)
            z_moments(PAIRS - 1, 1, 0)
            z_rows(PAIRS - 1, 1, 1)
            z_moments(PAIRS - 1, 1, 1)
            normalise_last(0)
            normalise_last(1)

        @block.tensor
        def _(pe):
            def turn_incidence(k, off):
                g = grp(k, off)
                wait(pe, inc_ready, g + 1)
                wait(pe, at_hi_ready, g)
                for j in range(G4):
                    last = nc.tensor.transpose(ps_adj[:, j * 64:(j + 1) * 64].bitcast(BF16), inc_bf[:, j],
                                               ident_bf[:, :])
                last.then_inc(inc_turned, 1)

            def sums(k, off):
                wait(pe, inc_t_ready, grp(k, off) + 1)
                wait(pe, group_w_ready, grp(k, off) + 1)
                for j in range(G4):
                    nc.tensor.matmul(ps_adj[:, j:j + 1], inc_bf[:, j], ones_bf[:, :], start=True, stop=True)
                for j in range(G4):
                    last = nc.tensor.matmul(ps_adj[:, G4 + 3 * j:G4 + 3 * j + 3], inc_t_bf[:, j],
                                            group_w[:, 3 * j:3 * j + 3], start=True, stop=True)
                last.then_inc(sums_done, 1)

            def turn_scaled(k, off):
                wait(pe, scaled_ready, grp(k, off) + 1)
                for j in range(G4):
                    last = nc.tensor.transpose(ps_adj[:, j * P:(j + 1) * P], scaled[:, j], ident[:, :])
                last.then_inc(scaled_turned, 1)

            def make_at(k, off):
                wait(pe, scaled_t_ready, grp(k, off) + 1)
                for j in range(G4):
                    last = nc.tensor.matmul(ps_adj[:, j * P:(j + 1) * P], inc_t[:, j], scaled_t[:, j],
                                            start=True, stop=True)
                last.then_inc(at_done, 1)

            def make_u(k, off):
                g, p = grp(k, off), off % 2
                wait(pe, at_ready, g + 1)
                wait(pe, x_in[p], loads(k, off))
                wait(pe, h_hi_ready, HB * g)
                for db in range(DB):
                    for j in range(G4):
                        last = nc.tensor.matmul(ps_hid[db][:, j * P:(j + 1) * P],
                                                x_sb[:, p, j, db * P:(db + 1) * P], at_sb[:, j],
                                                start=True, stop=True)
                    last.then_inc(u_done, 1)

            def hidden(k, off, hb):
                g = grp(k, off)
                cols = slice(hb * P, (hb + 1) * P)
                acc = ps_hid[hb % 2]
                if hb == 0:
                    wait(pe, u_lo_ready, DB * g + 1)
                    wait(pe, u_hi_ready, DB * g + DB)
                elif hb >= 2:
                    wait(pe, h_hi_ready, HB * g + hb - 1)
                terms = [(w, u_hi, db) for db in range(DB) for w in (w1_hi, w1_lo)]
                terms += [(w1_hi, u_lo, db) for db in range(DB)]
                for i, (w, u, db) in enumerate(terms):
                    if hb == 0 and i == len(terms) - 1:
                        wait(pe, u_lo_ready, DB * g + DB)
                    last = nc.tensor.matmul(acc[:, :], w[:, db, cols], u[:, db], start=(i == 0),
                                            stop=(i == len(terms) - 1))
                last.then_inc(hid_done, 1)

            def turn_h(k, off, b):
                n = G4 * grp(k, off) + b
                wait(pe, h_stats_ready, n - 1)
                for hb in range(HB):
                    if b == 0:
                        wait(pe, h_ready, HB * grp(k, off) + hb + 1)
                    last = nc.tensor.transpose(ps_ht[b % 2][:, hb * P:(hb + 1) * P],
                                               h_sb[:, hb, b * P:(b + 1) * P], ident[:, :])
                last.then_inc(ht_done, 1)

            def second(k, off, b):
                g = grp(k, off)
                nodes_b = slice(b * P, (b + 1) * P)
                acc = ps_v[b // 2][:, (b % 2) * d_in:(b % 2 + 1) * d_in]
                if b % 2 == 0:
                    wait(pe, v_ready, G4 * (g - 1) + b + 2)
                for hb in range(HB):
                    if b == 0:
                        wait(pe, h_hi_ready, HB * g + hb + 1)
                    terms = [(h_hi, w2_hi), (h_hi, w2_lo), (h_lo, w2_hi)]
                    for i, (h, w) in enumerate(terms):
                        if b == 0 and i == 2:
                            wait(pe, h_lo_ready, HB * g + hb + 1)
                        last = nc.tensor.matmul(acc, h[:, hb, nodes_b], w[:, hb], start=(hb == 0 and i == 0),
                                                stop=(hb == HB - 1 and i == 2))
                last.then_inc(v_done, 1)

            def mix(k, off, q):
                g, p = grp(k, off), off % 2
                wait(pe, v_hi_ready, 2 * g + q + 1)
                wait(pe, z_ready, 2 * g + q)
                wait(pe, v_lo_ready, 2 * g + q + 1)
                wait(pe, at_lo_ready, g + 1)
                for b in (2 * q, 2 * q + 1):
                    terms = [(at_hi, v_hi), (at_lo, v_hi), (at_hi, v_lo)]
                    for i, (a, v) in enumerate(terms):
                        last = nc.tensor.matmul(ps_y[:, (b % 2) * d_in:(b % 2 + 1) * d_in], a[:, p, b], v[:, b],
                                                start=(i == 0), stop=(i == len(terms) - 1))
                last.then_inc(y_done, 1)

            pe.wait_ge(consts, 2)
            turn_incidence(0, 0)
            pe.wait_ge(first_rows_in, 16)
            nc.tensor.transpose(ps_rows[:, 0:graphs], first_rows[:, :], ident[:, :]).then_inc(edge_turned, 1)
            pe.wait_ge(w1_in, 16)
            for db in range(DB):
                for hb in range(HB):
                    last = nc.tensor.transpose(ps_w[db][:, hb * P:(hb + 1) * P],
                                               w1_rows[:, hb, db * P:(db + 1) * P], ident[:, :])
            last.then_inc(w1_turned, 1)
            sums(0, 0)
            turn_scaled(0, 0)
            make_at(0, 0)
            pe.wait_ge(edge_split, 1)
            pe.wait_ge(b1_in, 16)
            nc.tensor.transpose(ps_rows[:, graphs:graphs + HB], b1_rows[:, :], ident[0:HB, 0:HB]
                                ).then_inc(b1_turned, 1)
            make_u(0, 0)
            pe.wait_ge(w1_lo_ready, DB)
            pe.wait_ge(w2_centring, 2 + DB)
            for hb in range(HB):
                for db in range(DB):
                    at = (hb % 2) * d_in + db * P
                    last = nc.tensor.transpose(ps_w[hb // 2][:, at:at + P],
                                               w2_centred[:, db, hb * P:(hb + 1) * P], ident[:, :])
            last.then_inc(w2_turned, 1)
            turn_incidence(0, 1)
            pe.wait_ge(t_prep, 2 * DB + 1)
            pe.wait_ge(b1_ready, 1)
            for db in range(DB):
                last = nc.tensor.matmul(ps_rows[:, db * P:(db + 1) * P], t_wide[:, db], ident[:, :],
                                        start=True, stop=True)
            last.then_inc(t_spread, 1)

            def iteration(k, off, first, last):
                if not (last or first):
                    sums(k, off + 1)
                hidden(k, off, 0)
                if first:
                    sums(k, off + 1)
                hidden(k, off, 1)
                if not first:
                    mix(k, off - 1, 0)
                hidden(k, off, 2)
                if not last:
                    turn_scaled(k, off + 1)
                hidden(k, off, 3)
                if not last:
                    make_at(k, off + 1)
                if first:
                    pe.wait_ge(w2_lo_ready, 2)
                    pe.wait_ge(t_ready, 1)
                turn_h(k, off, 0)
                turn_h(k, off, 1)
                second(k, off, 0)
                if not first:
                    mix(k, off - 1, 1)
                if not last:
                    make_u(k, off + 1)
                turn_h(k, off, 2)
                second(k, off, 1)
                turn_h(k, off, 3)
                if not (last or before_last(k, off)):
                    turn_incidence(k, off + 2)
                second(k, off, 2)
                second(k, off, 3)

            over_groups(pe, iteration)
            mix(PAIRS - 1, 1, 0)
            mix(PAIRS - 1, 1, 1)


_INS = ["x", "adj", "L0_gnn_W1", "L0_gnn_b1", "L0_gnn_gamma", "L0_gnn_beta", "L0_gnn_W2", "L0_gnn_b2"]


def kernel(**inputs):
    import numpy as np
    import concourse.bacc as bacc
    from concourse.bass_utils import run_bass_kernel_spmd as run

    nc = bacc.Bacc("TRN2", target_bir_lowering=False, num_devices=1)
    arrays, args = {}, []
    for name in _INS:
        a = np.ascontiguousarray(inputs[name])
        arrays[f"in_{name}"] = a
        args.append(nc.dram_tensor(f"in_{name}", a.shape, mybir.dt.from_np(a.dtype), kind="ExternalInput").ap())
    out = nc.dram_tensor("out", arrays["in_x"].shape, F32, kind="ExternalOutput").ap()
    hypergraph_block(nc, *args, out)
    r = run(nc, [arrays], core_ids=[0])
    return r.results[0]["out"]
```

```python
import concourse.bass as bass
from concourse import mybir
from contextlib import ExitStack

F32 = mybir.dt.float32
F32R = mybir.dt.float32r
BF16 = mybir.dt.bfloat16
ALU = mybir.AluOpType
ACT = mybir.ActivationFunctionType
AX = mybir.AxisListType

P = 128
LN_EPS = 1e-5
TINY = 1.1754944e-38


def hypergraph_block(nc, x, adj, w1, b1, gamma, beta, w2, b2, out):
    graphs, nodes, d_in = x.shape
    d_hid = w1.shape[0]
    assert nodes == P and d_in == w2.shape[0]
    DB = d_in // P
    HB = d_hid // P
    G4 = 512 // P
    GROUPS = graphs // G4
    PAIRS = GROUPS // 2

    ctx = ExitStack()
    with ctx:
        def sb(name, shape, dt=F32):
            return ctx.enter_context(nc.sbuf_tensor(name, shape, dt))

        def sem(name):
            return ctx.enter_context(nc.semaphore(name))

        ident = sb("ident", [P, P])
        ident_bf = sb("ident_bf", [P, P], BF16)
        ones_sq = sb("ones_sq", [P, P])
        ones_bf = sb("ones_bf", [P, 1], BF16)
        minus_half = sb("minus_half", [P, 2])
        eps = sb("eps", [P, 2])
        zeros = sb("zeros", [P, 2])
        w1_rows = sb("w1_rows", [P, HB, d_in])
        w2_rows = sb("w2_rows", [P, DB, d_hid])
        w2_scaled = sb("w2_scaled", [P, DB, d_hid])
        w2_centred = sb("w2_centred", [P, DB, d_hid])
        w2_beta = sb("w2_beta", [P, DB, d_hid])
        gamma_all = sb("gamma_all", [P, d_hid])
        beta_all = sb("beta_all", [P, d_hid])
        b2_all = sb("b2_all", [P, d_in])
        b1_rows = sb("b1_rows", [HB, P])
        first_rows = sb("first_rows", [P, P])
        w2_sum = sb("w2_sum", [P, DB])
        w2_mean = sb("w2_mean", [P, DB])
        t_col = sb("t_col", [P, DB])
        t_wide = sb("t_wide", [P, DB, P])
        b1_col = sb("b1_col", [P, HB])
        b2_half = sb("b2_half", [P, 2, d_in])
        t_all = sb("t_all", [P, d_in])
        edge_w = sb("edge_w", [P, graphs])
        edge_rest = sb("edge_rest", [P, 2, graphs])
        edge_parts = sb("edge_parts", [P, 3 * graphs], BF16)
        w1_hi = sb("w1_hi", [P, DB, d_hid], F32R)
        w1_lo = sb("w1_lo", [P, DB, d_hid], F32R)
        w2_hi = sb("w2_hi", [P, HB, d_in], F32R)
        w2_lo = sb("w2_lo", [P, HB, d_in], F32R)

        adj_sb = sb("adj_sb", [P, 2, G4, P])
        x_sb = sb("x_sb", [P, 2, G4, d_in])
        xb_sb = sb("xb_sb", [P, 2, G4, d_in])
        at_hi = sb("at_hi", [P, 2, G4, P], F32R)
        at_lo = sb("at_lo", [P, 2, G4, P], F32R)
        out_sb = sb("out_sb", [P, 2, G4, d_in])
        inc_bf = sb("inc_bf", [P, G4, P], BF16)
        inc_t = sb("inc_t", [P, G4, P], F32R)
        inc_t_bf = sb("inc_t_bf", [P, G4, P], BF16)
        group_w = sb("group_w", [P, 3 * G4], BF16)
        d_sum = sb("d_sum", [P, G4])
        safe = sb("safe", [P, 2 * G4])
        inv = sb("inv", [P, 2 * G4])
        d_pos = sb("d_pos", [P, G4])
        d_inv = sb("d_inv", [P, G4])
        scaled = sb("scaled", [P, G4, P])
        scaled_t = sb("scaled_t", [P, G4, 2, P], F32R)
        u_hi = sb("u_hi", [P, DB, G4 * P], F32R)
        u_lo = sb("u_lo", [P, DB, G4 * P], F32R)
        h_sb = sb("h_sb", [P, HB, G4 * P])
        h_hi = sb("h_hi", [P, HB, G4 * P], F32R)
        h_lo = sb("h_lo", [P, HB, G4 * P], F32R)
        at_part = sb("at_part", [P, G4, P])
        at_sb = sb("at_sb", [P, G4, P])
        v_sb = sb("v_sb", [P, G4, d_in])
        v_hi = sb("v_hi", [P, G4, d_in], F32R)
        v_lo = sb("v_lo", [P, G4, d_in], F32R)
        z_sb = sb("z_sb", [P, G4, d_in])
        h_stats = sb("h_stats", [P, G4, 6])
        h_mv = sb("h_mv", [P, G4, 2])
        h_var = sb("h_var", [P, G4])
        h_rstd = sb("h_rstd", [P, G4])
        z_stats = sb("z_stats", [P, G4, 6])
        z_mv = sb("z_mv", [P, G4, 2])
        z_var = sb("z_var", [P, G4])
        z_rstd = sb("z_rstd", [P, G4])
        z_scaled_mean = sb("z_scaled_mean", [P, G4])
        z_shift = sb("z_shift", [P, G4])

        bank = [ctx.enter_context(nc.psum_tensor(f"bank{i}", [P, 512], F32)) for i in range(8)]
        ps_hid = bank[0:2]
        ps_v = bank[2:4]
        ps_ht = bank[4:6]
        ps_adj = bank[6]
        ps_at = (bank[6], bank[5])
        ps_y = bank[7]

        ps_edge = bank[5]
        ps_rows = bank[7]
        ps_w = bank[3:5]

        first_rows_in = sem("first_rows_in")
        w1_in = sem("w1_in")
        w2_in = sem("w2_in")
        gamma_in = sem("gamma_in")
        beta_in = sem("beta_in")
        b1_in = sem("b1_in")
        b2_in = sem("b2_in")
        adj_in = [sem(f"adj_in{p}") for p in range(2)]
        x_in = [sem(f"x_in{p}") for p in range(2)]
        stored = [sem(f"stored{p}") for p in range(2)]
        zeroed = sem("zeroed")
        consts = sem("consts")
        edge_turned = sem("edge_turned")
        edge_split = sem("edge_split")
        w1_turned = sem("w1_turned")
        w1_hi_ready = sem("w1_hi_ready")
        w1_lo_ready = sem("w1_lo_ready")
        b2_ready = sem("b2_ready")
        b1_turned = sem("b1_turned")
        b1_ready = sem("b1_ready")
        w2_scaling = sem("w2_scaling")
        w2_centring = sem("w2_centring")
        w2_turned = sem("w2_turned")
        w2_hi_ready = sem("w2_hi_ready")
        w2_lo_ready = sem("w2_lo_ready")
        t_prep = sem("t_prep")
        t_spread = sem("t_spread")
        t_ready = sem("t_ready")
        inc_turned = sem("inc_turned")
        sums_done = sem("sums_done")
        scaled_turned = sem("scaled_turned")
        at_done = sem("at_done")
        u_done = sem("u_done")
        hid_done = sem("hid_done")
        ht_done = sem("ht_done")
        v_done = sem("v_done")
        y_done = sem("y_done")
        inc_t_ready = sem("inc_t_ready")
        scaled_ready = sem("scaled_ready")
        at_part_ready = sem("at_part_ready")
        at_hi_ready = sem("at_hi_ready")
        v_hi_ready = sem("v_hi_ready")
        u_hi_ready = sem("u_hi_ready")
        h_ready = sem("h_ready")
        h_hi_ready = sem("h_hi_ready")
        inc_ready = sem("inc_ready")
        d_summed = sem("d_summed")
        sums_safe = sem("sums_safe")
        inv_ready = sem("inv_ready")
        d_inv_ready = sem("d_inv_ready")
        scaled_t_hi_ready = sem("scaled_t_hi_ready")
        scaled_t_lo_ready = sem("scaled_t_lo_ready")
        at_ready = sem("at_ready")
        u_lo_ready = sem("u_lo_ready")
        h_lo_ready = sem("h_lo_ready")
        h_stats_ready = sem("h_stats_ready")
        stats_seen = sem("stats_seen")
        h_mv_ready = sem("h_mv_ready")
        v_ready = sem("v_ready")
        z_ready = sem("z_ready")
        z_stats_ready = sem("z_stats_ready")
        z_mv_ready = sem("z_mv_ready")
        out_ready = sem("out_ready")
        group_w_ready = sem("group_w_ready")
        xb_ready = sem("xb_ready")
        at_lo_ready = sem("at_lo_ready")
        v_lo_ready = sem("v_lo_ready")
        h_eps = sem("h_eps")
        h_rstd_ready = sem("h_rstd_ready")
        z_eps = sem("z_eps")
        z_rstd_ready = sem("z_rstd_ready")
        z_mean_scaled = sem("z_mean_scaled")
        z_shift_ready = sem("z_shift_ready")

        adj_dram = adj.rearrange("n i e -> i n e")
        x_dram = x.rearrange("n c d -> c n d")
        out_dram = out.rearrange("n c d -> c n d")

        def wait(eng, s, value):
            if not isinstance(value, int) or value > 0:
                eng.wait_ge(s, value)

        def grp(k, off):
            return 2 * k + off

        def graph0(k, off):
            return 2 * G4 * k + G4 * off

        def loads(k, off):
            return 16 * k + 16 * (off // 2 + 1)

        def before_last(k, off):
            return isinstance(k, int) and k == PAIRS - 1 and off == 0

        def over_groups(eng, iteration):
            iteration(0, 0, True, False)
            iteration(0, 1, False, False)
            with eng.Fori(1, PAIRS - 1) as k:
                for off in range(2):
                    iteration(k, off, False, False)
            iteration(PAIRS - 1, 0, False, False)
            iteration(PAIRS - 1, 1, False, True)

        block = ctx.enter_context(nc.Block())

        @block.sync
        def _(sp):
            def load_adj(k, off):
                sp.dma_start(adj_sb[:, off % 2], adj_dram[:, bass.ds(graph0(k, off), G4)]
                             ).then_inc(adj_in[off % 2], 16)

            def load_x(k, off):
                sp.dma_start(x_sb[:, off % 2], x_dram[:, bass.ds(graph0(k, off), G4)]
                             ).then_inc(x_in[off % 2], 16)

            def store(k, off):
                wait(sp, out_ready, G4 * (grp(k, off) + 1))
                sp.dma_start(out_dram[:, bass.ds(graph0(k, off), G4)], out_sb[:, off % 2]
                             ).then_inc(stored[off % 2], 16)

            sp.dma_start(first_rows[:, :], adj[:, 0, :]).then_inc(first_rows_in, 16)
            load_adj(0, 0)
            sp.dma_start(w1_rows[:, :, :], w1.rearrange("(b p) d -> p b d", p=P)).then_inc(w1_in, 16)
            load_x(0, 0)
            sp.dma_start(b1_rows[:, :], b1.rearrange("(b p) -> b p", p=P)).then_inc(b1_in, 16)
            sp.dma_start(w2_rows[:, :, :], w2.rearrange("(b p) h -> p b h", p=P)).then_inc(w2_in, 16)
            for row, values, arrived in ((gamma_all, gamma, gamma_in), (beta_all, beta, beta_in),
                                         (b2_all, b2, b2_in)):
                sp.dma_start(row[:, :], values.partition_broadcast(P)).then_inc(arrived, 16)
            load_adj(0, 1)
            load_x(0, 1)

            def iteration(k, off, first, last):
                g = grp(k, off)
                if not (last or before_last(k, off)):
                    wait(sp, inc_ready, g + 1)
                    load_adj(k, off + 2)
                if not (isinstance(k, int) and k == 0):
                    store(k, off - 2)
                if not (last or before_last(k, off)):
                    wait(sp, u_done, DB * (g + 1))
                    wait(sp, xb_ready, 2 * (g + 1))
                    load_x(k, off + 2)

            over_groups(sp, iteration)
            store(PAIRS - 1, 0)
            p, n0 = 1, graphs - G4
            for q in range(2):
                sp.wait_ge(out_ready, n0 + 2 * q + 2)
                sp.dma_start(out_dram[:, n0 + 2 * q:n0 + 2 * q + 2], out_sb[:, p, 2 * q:2 * q + 2]
                             ).then_inc(stored[p], 16)
            sp.wait_ge(stored[0], 16 * PAIRS)
            sp.wait_ge(stored[1], 16 * PAIRS + 16)

        @block.gpsimd
        def _(pool):
            nc.gpsimd.memset(ident[:, :], 0.0).then_inc(zeroed, 1)
            nc.gpsimd.memset(ident_bf[:, :], 0.0).then_inc(zeroed, 1)
            nc.gpsimd.memset(ones_sq[:, :], 1.0)
            nc.gpsimd.memset(ones_bf[:, :], 1.0)
            nc.gpsimd.memset(minus_half[:, :], -0.5)
            nc.gpsimd.memset(eps[:, :], LN_EPS)
            nc.gpsimd.memset(zeros[:, :], 0.0)
            pool.wait_ge(zeroed, 2)
            for m in (ident, ident_bf):
                nc.gpsimd.affine_select(out=m[:, :], in_=m[:, :], compare_op=ALU.not_equal, fill=1.0,
                                        base=0, pattern=[[-1, P]], channel_multiplier=1).then_inc(consts, 1)

            def residual(k, off, q):
                g, p = grp(k, off), off % 2
                wait(pool, x_in[p], loads(k, off))
                wait(pool, z_ready, 2 * (g - 2) + q + 1)
                nc.gpsimd.tensor_tensor(xb_sb[:, p, 2 * q:2 * q + 2], x_sb[:, p, 2 * q:2 * q + 2],
                                        b2_half[:, :, :], ALU.add).then_inc(xb_ready, 1)

            def edge_columns(k, off):
                g = grp(k, off)
                wait(pool, sums_done, g)
                nc.gpsimd.tensor_copy(group_w[:, :], edge_parts[:, bass.ds(3 * graph0(k, off), 3 * G4)]
                                      ).then_inc(group_w_ready, 1)

            def rstd(k, off, q, mv, mv_ready, var, eps_done, r, r_ready):
                n = 2 * grp(k, off) + q
                cols = slice(2 * q, 2 * q + 2)
                wait(pool, mv_ready, 2 * n + 2)
                nc.gpsimd.tensor_tensor(var[:, cols], mv[:, cols, 1], eps[:, :], ALU.add
                                        ).then_inc(eps_done, 1)
                wait(pool, eps_done, n + 1)
                nc.gpsimd.tensor_tensor(r[:, cols], var[:, cols], minus_half[:, :], ALU.pow
                                        ).then_inc(r_ready, 1)

            def low_at(k, off):
                g, p = grp(k, off), off % 2
                wait(pool, at_hi_ready, g + 1)
                wait(pool, y_done, G4 * (g - 1))
                nc.gpsimd.tensor_tensor(at_lo[:, p], at_sb[:, :], at_hi[:, p].bitcast(F32), ALU.subtract
                                        ).then_inc(at_lo_ready, 1)

            def low_v(k, off, q):
                g, n = grp(k, off), 2 * grp(k, off) + q
                rows = slice(2 * q, 2 * q + 2)
                wait(pool, v_hi_ready, n + 1)
                wait(pool, y_done, G4 * (g - 1) + 2 * q + 2)
                nc.gpsimd.tensor_tensor(v_lo[:, rows], v_sb[:, rows], v_hi[:, rows].bitcast(F32), ALU.subtract
                                        ).then_inc(v_lo_ready, 1)

            def h_scale(k, off, q):
                wait(pool, v_ready, G4 * (grp(k, off) - 1) + 2 * q + 2)
                rstd(k, off, q, h_mv, h_mv_ready, h_var, h_eps, h_rstd, h_rstd_ready)

            def z_scale(k, off, q):
                wait(pool, out_ready, G4 * (grp(k, off) - 1) + 2 * q + 2)
                rstd(k, off, q, z_mv, z_mv_ready, z_var, z_eps, z_rstd, z_rstd_ready)
                if isinstance(k, int) and grp(k, off) == GROUPS - 1:
                    return
                n, cols = 2 * grp(k, off) + q, slice(2 * q, 2 * q + 2)
                wait(pool, z_rstd_ready, n + 1)
                nc.gpsimd.tensor_tensor(z_scaled_mean[:, cols], z_mv[:, cols, 0], z_rstd[:, cols], ALU.mult
                                        ).then_inc(z_mean_scaled, 1)
                wait(pool, z_mean_scaled, n + 1)
                nc.gpsimd.tensor_tensor(z_shift[:, cols], zeros[:, :], z_scaled_mean[:, cols], ALU.subtract
                                        ).then_inc(z_shift_ready, 1)

            pool.wait_ge(edge_split, 6)
            edge_columns(0, 0)
            edge_columns(0, 1)
            for row, arrived, product, done in ((gamma_all, gamma_in, w2_scaled, w2_scaling),
                                                (beta_all, beta_in, w2_beta, t_prep)):
                pool.wait_ge(w2_in, 16)
                pool.wait_ge(arrived, 16)
                for db in range(DB):
                    nc.gpsimd.tensor_tensor(product[:, db], w2_rows[:, db], row[:, :], ALU.mult
                                            ).then_inc(done, 1)
            low_at(0, 0)
            pool.wait_ge(b2_ready, 2)
            residual(0, 0, 0)
            residual(0, 0, 1)

            def iteration(k, off, first, last):
                if not (last or before_last(k, off)):
                    edge_columns(k, off + 2)
                if not first:
                    low_v(k, off - 1, 0)
                    low_v(k, off - 1, 1)
                if not last:
                    residual(k, off + 1, 0)
                    low_at(k, off + 1)
                    residual(k, off + 1, 1)
                if not first:
                    z_scale(k, off - 1, 0)
                h_scale(k, off, 0)
                if not first:
                    z_scale(k, off - 1, 1)
                h_scale(k, off, 1)

            over_groups(pool, iteration)
            z_scale(PAIRS - 1, 1, 0)
            z_scale(PAIRS - 1, 1, 1)

        @block.scalar
        def _(act):
            def h_block(k, off, hb):
                g = grp(k, off)
                wait(act, hid_done, HB * g + hb + 1)
                if hb == 0:
                    wait(act, v_done, G4 * g)
                    wait(act, ht_done, G4 * g)
                    wait(act, h_lo_ready, HB * g)
                nc.scalar.activation(h_sb[:, hb], ps_hid[hb % 2][:, :], ACT.Relu, bias=b1_col[:, hb:hb + 1]
                                     ).then_inc(h_ready, 1)
                nc.scalar.activation(h_hi[:, hb], ps_hid[hb % 2][:, :], ACT.Relu, bias=b1_col[:, hb:hb + 1]
                                     ).then_inc(h_hi_ready, 1)

            def copy_inc_t(k, off):
                g = grp(k, off)
                wait(act, inc_turned, g + 1)
                wait(act, at_done, g)
                nc.scalar.activation(inc_t_bf[:, :, :], ps_adj[:, 0:256].bitcast(BF16), ACT.Copy)
                nc.scalar.activation(inc_t[:, :, :], ps_adj[:, 0:256].bitcast(BF16), ACT.Copy
                                     ).then_inc(inc_t_ready, 1)

            def scale(k, off):
                g = grp(k, off)
                wait(act, d_inv_ready, g + 1)
                wait(act, scaled_turned, g)
                for j in range(G4):
                    last = nc.scalar.activation(scaled[:, j], inc_bf[:, j], ACT.Copy, scale=d_inv[:, j:j + 1])
                last.then_inc(scaled_ready, 1)

            def copy_at_part(k, off):
                g = grp(k, off)
                wait(act, at_done, g + 1)
                wait(act, at_ready, 2 * g)
                for i in range(2):
                    both = ps_at[i][:, :].rearrange("p (j w n) -> p j w n", w=2, n=P)
                    nc.scalar.activation(at_part[:, 2 * i:2 * i + 2], both[:, :, 0], ACT.Copy
                                         ).then_inc(at_part_ready, 1)

            def at_high(k, off):
                g = grp(k, off)
                wait(act, at_ready, 2 * g + 2)
                wait(act, y_done, G4 * (g - 1))
                nc.scalar.activation(at_hi[:, off % 2], at_sb[:, :], ACT.Copy).then_inc(at_hi_ready, 1)

            def v_high(k, off, q):
                g, rows = grp(k, off), slice(2 * q, 2 * q + 2)
                wait(act, v_ready, G4 * g + 2 * q + 2)
                wait(act, y_done, G4 * (g - 1) + 2 * q + 2)
                nc.scalar.activation(v_hi[:, rows], v_sb[:, rows], ACT.Copy).then_inc(v_hi_ready, 1)

            def u_high(k, off):
                g = grp(k, off)
                wait(act, hid_done, HB * g)
                for db in range(DB):
                    wait(act, u_done, DB * g + db + 1)
                    nc.scalar.activation(u_hi[:, db], ps_hid[db][:, :], ACT.Copy).then_inc(u_hi_ready, 1)

            def normalise(k, off, q):
                g, p = grp(k, off), off % 2
                wait(act, z_shift_ready, 2 * g + q + 1)
                wait(act, stored[p], loads(k, off - 2))
                for b in (2 * q, 2 * q + 1):
                    nc.scalar.activation(out_sb[:, p, b], z_sb[:, b], ACT.Identity, scale=z_rstd[:, b:b + 1],
                                         bias=z_shift[:, b:b + 1]).then_inc(out_ready, 1)

            act.wait_ge(edge_turned, 1)
            nc.scalar.activation(edge_w[:, :], ps_edge[:, 0:graphs], ACT.Copy).then_inc(edge_split, 1)
            copy_inc_t(0, 0)
            act.wait_ge(w1_turned, 1)
            for db in range(DB):
                nc.scalar.activation(w1_hi[:, db], ps_w[db][:, :], ACT.Copy).then_inc(w1_hi_ready, 1)
            scale(0, 0)
            act.wait_ge(b2_in, 16)
            for a in range(2):
                nc.scalar.activation(b2_half[:, a], b2_all[:, :], ACT.Copy, scale=0.5).then_inc(b2_ready, 1)
            copy_at_part(0, 0)
            at_high(0, 0)
            u_high(0, 0)
            copy_inc_t(0, 1)
            act.wait_ge(w2_turned, 1)
            for i in range(2):
                nc.scalar.activation(w2_hi[:, 2 * i:2 * i + 2], ps_w[i][:, :], ACT.Copy).then_inc(w2_hi_ready, 1)
            act.wait_ge(b1_ready, 1)

            def iteration(k, off, first, last):
                if not first:
                    v_high(k, off - 1, 0)
                h_block(k, off, 0)
                if first:
                    scale(k, off + 1)
                h_block(k, off, 1)
                if not first:
                    v_high(k, off - 1, 1)
                if not (first or last):
                    copy_at_part(k, off + 1)
                h_block(k, off, 2)
                h_block(k, off, 3)
                if first:
                    copy_at_part(k, off + 1)
                if not last:
                    at_high(k, off + 1)
                if not (last or before_last(k, off)):
                    copy_inc_t(k, off + 2)
                if not last:
                    u_high(k, off + 1)
                if not first:
                    normalise(k, off - 1, 0)
                if not (last or before_last(k, off)):
                    scale(k, off + 2)
                if not first:
                    normalise(k, off - 1, 1)

            over_groups(act, iteration)
            v_high(PAIRS - 1, 1, 0)
            v_high(PAIRS - 1, 1, 1)

        @block.vector
        def _(dve):
            def incidence(k, off):
                g, p = grp(k, off), off % 2
                wait(dve, adj_in[p], loads(k, off))
                wait(dve, inc_turned, g)
                wait(dve, scaled_ready, g)
                nc.vector.tensor_scalar(inc_bf[:, :, :], adj_sb[:, p], 0.0, None, ALU.not_equal
                                        ).then_inc(inc_ready, 1)

            def inverses(k, off):
                g = grp(k, off)
                wait(dve, sums_done, g + 1)
                wait(dve, scaled_t_lo_ready, g)
                wait(dve, scaled_ready, g)
                nc.vector.tensor_scalar(safe[:, 0:G4], ps_adj[:, 0:G4], 1.0, None, ALU.max).then_inc(sums_safe, 1)
                nc.vector.tensor_reduce(d_sum[:, :], ps_adj[:, G4:G4 + 3 * G4].rearrange("p (j w) -> p j w", w=3),
                                        AX.X, ALU.add).then_inc(d_summed, 1)
                wait(dve, d_summed, g + 1)
                nc.vector.tensor_scalar(safe[:, G4:2 * G4], d_sum[:, :], TINY, None, ALU.max
                                        ).then_inc(sums_safe, 1)
                nc.vector.tensor_scalar(d_pos[:, :], d_sum[:, :], 0.0, None, ALU.is_gt
                                        ).then_inc(sums_safe, 1)
                wait(dve, sums_safe, 3 * g + 3)
                nc.vector.reciprocal(inv[:, :], safe[:, :]).then_inc(inv_ready, 1)
                wait(dve, inv_ready, g + 1)
                nc.vector.tensor_tensor(d_inv[:, :], inv[:, G4:2 * G4], d_pos[:, :], ALU.mult
                                        ).then_inc(d_inv_ready, 1)

            def scale_t(k, off):
                g = grp(k, off)
                wait(dve, scaled_turned, g + 1)
                wait(dve, at_done, g)
                nc.vector.tensor_tensor(scaled_t[:, :, 0], ps_adj[:, :].rearrange("p (j i) -> p j i", i=P),
                                        inv[:, 0:G4].unsqueeze(2).broadcast_to([P, G4, P]), ALU.mult
                                        ).then_inc(scaled_t_hi_ready, 1)
                wait(dve, scaled_t_hi_ready, g + 1)
                for j in range(G4):
                    last = nc.vector.scalar_tensor_tensor(scaled_t[:, j, 1], ps_adj[:, j * P:(j + 1) * P],
                                                          inv[:, j:j + 1], scaled_t[:, j, 0].bitcast(F32),
                                                          ALU.mult, ALU.subtract)
                last.then_inc(scaled_t_lo_ready, 1)

            def add_at(k, off):
                g = grp(k, off)
                wait(dve, u_done, DB * g)
                wait(dve, at_hi_ready, g)
                wait(dve, at_lo_ready, g)
                for i in range(2):
                    both = ps_at[i][:, :].rearrange("p (j w n) -> p j w n", w=2, n=P)
                    wait(dve, at_part_ready, 2 * g + i + 1)
                    nc.vector.tensor_tensor(at_sb[:, 2 * i:2 * i + 2], both[:, :, 1],
                                            at_part[:, 2 * i:2 * i + 2], ALU.add).then_inc(at_ready, 1)

            def u_low(k, off, db):
                wait(dve, u_hi_ready, DB * grp(k, off) + db + 1)
                nc.vector.tensor_tensor(u_lo[:, db], ps_hid[db][:, :], u_hi[:, db].bitcast(F32),
                                        ALU.subtract).then_inc(u_lo_ready, 1)

            def h_low(k, off, hb):
                g = grp(k, off)
                wait(dve, h_ready, HB * g + hb + 1)
                wait(dve, h_hi_ready, HB * g + hb + 1)
                nc.vector.tensor_tensor(h_lo[:, hb], h_sb[:, hb], h_hi[:, hb].bitcast(F32),
                                        ALU.subtract).then_inc(h_lo_ready, 1)

            def h_moments(k, off, b):
                n = G4 * grp(k, off) + b
                wait(dve, ht_done, n + 1)
                wait(dve, h_rstd_ready, 2 * (grp(k, off) - 1) + b // 2 + 1)
                nc.vector.bn_stats(h_stats[:, b], ps_ht[b % 2][:, :]).then_inc(h_stats_ready, 1)

            def h_variance(k, off, b):
                wait(dve, h_stats_ready, G4 * grp(k, off) + b + 1)
                dve.sem_inc(stats_seen, 1)
                nc.vector.bn_aggr(h_mv[:, b], h_stats[:, b]).then_inc(h_mv_ready, 1)

            def v_rows(k, off, q):
                g = grp(k, off)
                wait(dve, h_rstd_ready, 2 * g + q + 1)
                wait(dve, v_done, G4 * g + 2 * q + 2)
                wait(dve, v_lo_ready, 2 * (g - 1) + q + 1)
                for b in (2 * q, 2 * q + 1):
                    nc.vector.scalar_tensor_tensor(v_sb[:, b], ps_v[q][:, (b % 2) * d_in:(b % 2 + 1) * d_in],
                                                   h_rstd[:, b:b + 1], t_all[:, :], ALU.mult, ALU.add
                                                   ).then_inc(v_ready, 1)

            def z_rows(k, off, q):
                g, p, n = grp(k, off), off % 2, 2 * grp(k, off) + q
                wait(dve, y_done, 2 * n + 2)
                wait(dve, xb_ready, n + 1)
                wait(dve, out_ready, G4 * (g - 1) + 2 * q + 2)
                nc.vector.scalar_tensor_tensor(z_sb[:, 2 * q:2 * q + 2].rearrange("p a d -> p (a d)"),
                                               xb_sb[:, p, 2 * q:2 * q + 2].rearrange("p a d -> p (a d)"),
                                               2.0, ps_y[:, :], ALU.mult, ALU.add).then_inc(z_ready, 1)

            def z_moments(k, off, q):
                g, n = grp(k, off), 2 * grp(k, off) + q
                wait(dve, z_ready, n + 1)
                wait(dve, z_rstd_ready, 2 * (g - 1) + q + 1)
                for b in (2 * q, 2 * q + 1):
                    nc.vector.bn_stats(z_stats[:, b], z_sb[:, b]).then_inc(z_stats_ready, 1)

            def z_variances(k, off, q):
                g = grp(k, off)
                for b in (2 * q, 2 * q + 1):
                    wait(dve, z_stats_ready, G4 * g + b + 1)
                    dve.sem_inc(stats_seen, 1)
                    nc.vector.bn_aggr(z_mv[:, b], z_stats[:, b]).then_inc(z_mv_ready, 1)

            incidence(0, 0)
            dve.wait_ge(edge_split, 1)
            parts = edge_parts[:, :].rearrange("p (n w) -> p w n", w=3)
            rest = edge_w[:, :]
            for i in range(3):
                nc.vector.tensor_copy(parts[:, i], rest).then_inc(edge_split, 1)
                if i < 2:
                    dve.wait_ge(edge_split, 2 * i + 2)
                    nc.vector.tensor_tensor(edge_rest[:, i], rest, parts[:, i], ALU.subtract).then_inc(edge_split, 1)
                    dve.wait_ge(edge_split, 2 * i + 3)
                    rest = edge_rest[:, i]
            inverses(0, 0)
            scale_t(0, 0)
            dve.wait_ge(w1_hi_ready, DB)
            for db in range(DB):
                nc.vector.tensor_tensor(w1_lo[:, db], ps_w[db][:, :], w1_hi[:, db].bitcast(F32),
                                        ALU.subtract).then_inc(w1_lo_ready, 1)
            add_at(0, 0)
            dve.wait_ge(w2_scaling, DB)
            nc.vector.tensor_reduce(w2_sum[:, :], w2_scaled[:, :, :], AX.X, ALU.add).then_inc(w2_centring, 1)
            incidence(0, 1)
            dve.wait_ge(b1_turned, 1)
            nc.vector.tensor_copy(b1_col[:, :], ps_rows[:, 0:HB]).then_inc(b1_ready, 1)
            dve.wait_ge(w2_centring, 1)
            nc.vector.tensor_scalar(w2_mean[:, :], w2_sum[:, :], 1.0 / d_hid, None, ALU.mult
                                    ).then_inc(w2_centring, 1)
            dve.wait_ge(w2_centring, 2)
            for db in range(DB):
                nc.vector.tensor_scalar(w2_centred[:, db], w2_scaled[:, db], w2_mean[:, db:db + 1], None,
                                        ALU.subtract).then_inc(w2_centring, 1)
            for db in range(DB):
                u_low(0, 0, db)
            inverses(0, 1)
            dve.wait_ge(w2_hi_ready, 2)
            for i in range(2):
                nc.vector.tensor_tensor(w2_lo[:, 2 * i:2 * i + 2], ps_w[i][:, :],
                                        w2_hi[:, 2 * i:2 * i + 2].bitcast(F32), ALU.subtract
                                        ).then_inc(w2_lo_ready, 1)

            def beta_sums():
                dve.wait_ge(t_prep, DB)
                nc.vector.tensor_reduce(t_col[:, :], w2_beta[:, :, :], AX.X, ALU.add).then_inc(t_prep, 1)
                dve.wait_ge(t_prep, DB + 1)
                for db in range(DB):
                    nc.vector.tensor_scalar(t_wide[:, db], ones_sq[:, :], t_col[:, db:db + 1], None, ALU.mult
                                            ).then_inc(t_prep, 1)

            def keep_t():
                dve.wait_ge(t_spread, 1)
                nc.vector.tensor_copy(t_all[:, :], ps_rows[:, 0:d_in]).then_inc(t_ready, 1)
                dve.wait_ge(t_ready, 1)

            def low_v_last(q):
                rows = slice(2 * q, 2 * q + 2)
                dve.wait_ge(v_hi_ready, 2 * (GROUPS - 1) + q + 1)
                dve.wait_ge(y_done, G4 * (GROUPS - 2) + 2 * q + 2)
                nc.vector.tensor_tensor(v_lo[:, rows], v_sb[:, rows], v_hi[:, rows].bitcast(F32), ALU.subtract
                                        ).then_inc(v_lo_ready, 1)

            def normalise_last(q):
                dve.wait_ge(z_rstd_ready, 2 * (GROUPS - 1) + q + 1)
                dve.wait_ge(stored[1], 16 * (PAIRS - 1))
                for b in (2 * q, 2 * q + 1):
                    nc.vector.tensor_scalar(out_sb[:, 1, b], z_sb[:, b], z_mv[:, b, 0:1], z_rstd[:, b:b + 1],
                                            ALU.subtract, ALU.mult).then_inc(out_ready, 1)

            def iteration(k, off, first, last):
                if not first:
                    u_low(k, off, 1)
                if not (first or last):
                    scale_t(k, off + 1)
                if not first:
                    v_rows(k, off - 1, 1)
                wait(dve, v_done, G4 * grp(k, off))
                h_low(k, off, 0)
                if first:
                    scale_t(k, off + 1)
                else:
                    z_rows(k, off - 1, 0)
                h_low(k, off, 1)
                if not (first or last):
                    add_at(k, off + 1)
                if not first:
                    z_moments(k, off - 1, 0)
                if not (last or before_last(k, off)):
                    incidence(k, off + 2)
                h_low(k, off, 2)
                if not first:
                    z_variances(k, off - 1, 0)
                if first or last:
                    h_low(k, off, 3)
                h_moments(k, off, 0)
                if first:
                    add_at(k, off + 1)
                else:
                    z_rows(k, off - 1, 1)
                h_moments(k, off, 1)
                h_variance(k, off, 0)
                if not (first or last):
                    h_low(k, off, 3)
                h_variance(k, off, 1)
                if first:
                    beta_sums()
                if not first:
                    z_moments(k, off - 1, 1)
                if not last:
                    u_low(k, off + 1, 0)
                if not first:
                    z_variances(k, off - 1, 1)
                if not (last or before_last(k, off)):
                    inverses(k, off + 2)
                h_moments(k, off, 2)
                h_moments(k, off, 3)
                h_variance(k, off, 2)
                h_variance(k, off, 3)
                if first:
                    keep_t()
                v_rows(k, off, 0)

            over_groups(dve, iteration)
            low_v_last(0)
            v_rows(PAIRS - 1, 1, 1)
            z_rows(PAIRS - 1, 1, 0)
            low_v_last(1)
            z_moments(PAIRS - 1, 1, 0)
            z_variances(PAIRS - 1, 1, 0)
            z_rows(PAIRS - 1, 1, 1)
            z_moments(PAIRS - 1, 1, 1)
            z_variances(PAIRS - 1, 1, 1)
            normalise_last(0)
            normalise_last(1)

        @block.tensor
        def _(pe):
            def turn_incidence(k, off):
                g = grp(k, off)
                wait(pe, inc_ready, g + 1)
                wait(pe, at_ready, 2 * g - 1)
                for j in range(G4):
                    last = nc.tensor.transpose(ps_adj[:, j * 64:(j + 1) * 64].bitcast(BF16), inc_bf[:, j],
                                               ident_bf[:, :])
                last.then_inc(inc_turned, 1)

            def sums(k, off):
                wait(pe, inc_t_ready, grp(k, off) + 1)
                wait(pe, group_w_ready, grp(k, off) + 1)
                for j in range(G4):
                    nc.tensor.matmul(ps_adj[:, j:j + 1], inc_bf[:, j], ones_bf[:, :], start=True, stop=True)
                for j in range(G4):
                    last = nc.tensor.matmul(ps_adj[:, G4 + 3 * j:G4 + 3 * j + 3], inc_t_bf[:, j],
                                            group_w[:, 3 * j:3 * j + 3], start=True, stop=True)
                last.then_inc(sums_done, 1)

            def turn_scaled(k, off):
                wait(pe, scaled_ready, grp(k, off) + 1)
                for j in range(G4):
                    last = nc.tensor.transpose(ps_adj[:, j * P:(j + 1) * P], scaled[:, j], ident[:, :])
                last.then_inc(scaled_turned, 1)

            def make_at(k, off):
                g = grp(k, off)
                wait(pe, scaled_t_lo_ready, g + 1)
                wait(pe, h_stats_ready, G4 * (g - 1))
                for j in range(G4):
                    last = nc.tensor.matmul(ps_at[j // 2][:, (j % 2) * 2 * P:(j % 2 + 1) * 2 * P], inc_t[:, j],
                                            scaled_t[:, j].rearrange("p w n -> p (w n)"), start=True, stop=True)
                last.then_inc(at_done, 1)

            def make_u(k, off):
                g, p = grp(k, off), off % 2
                wait(pe, at_ready, 2 * g + 2)
                wait(pe, x_in[p], loads(k, off))
                wait(pe, h_hi_ready, HB * g)
                for db in range(DB):
                    for j in range(G4):
                        last = nc.tensor.matmul(ps_hid[db][:, j * P:(j + 1) * P],
                                                x_sb[:, p, j, db * P:(db + 1) * P], at_sb[:, j],
                                                start=True, stop=True)
                    last.then_inc(u_done, 1)

            def hidden(k, off, hb):
                g = grp(k, off)
                cols = slice(hb * P, (hb + 1) * P)
                acc = ps_hid[hb % 2]
                if hb == 0:
                    wait(pe, u_lo_ready, DB * g + 1)
                    wait(pe, u_hi_ready, DB * g + DB)
                elif hb >= 2:
                    wait(pe, h_hi_ready, HB * g + hb - 1)
                terms = [(w, u_hi, db) for db in range(DB) for w in (w1_hi, w1_lo)]
                terms += [(w1_hi, u_lo, db) for db in range(DB)]
                for i, (w, u, db) in enumerate(terms):
                    if hb == 0 and i == len(terms) - 1:
                        wait(pe, u_lo_ready, DB * g + DB)
                    last = nc.tensor.matmul(acc[:, :], w[:, db, cols], u[:, db], start=(i == 0),
                                            stop=(i == len(terms) - 1))
                last.then_inc(hid_done, 1)

            def turn_h(k, off, b):
                g, n = grp(k, off), G4 * grp(k, off) + b
                if b == 1 and not (isinstance(k, int) and g == GROUPS - 1):
                    wait(pe, at_ready, 2 * (g + 1) + 2)
                wait(pe, h_stats_ready, n - 1)
                for hb in range(HB):
                    if b == 0:
                        wait(pe, h_ready, HB * grp(k, off) + hb + 1)
                    last = nc.tensor.transpose(ps_ht[b % 2][:, hb * P:(hb + 1) * P],
                                               h_sb[:, hb, b * P:(b + 1) * P], ident[:, :])
                last.then_inc(ht_done, 1)

            def second(k, off, b):
                g = grp(k, off)
                nodes_b = slice(b * P, (b + 1) * P)
                acc = ps_v[b // 2][:, (b % 2) * d_in:(b % 2 + 1) * d_in]
                if b % 2 == 0:
                    wait(pe, v_ready, G4 * (g - 1) + b + 2)
                for hb in range(HB):
                    if b == 0:
                        wait(pe, h_hi_ready, HB * g + hb + 1)
                    terms = [(h_hi, w2_hi), (h_hi, w2_lo), (h_lo, w2_hi)]
                    for i, (h, w) in enumerate(terms):
                        if b == 0 and i == 2:
                            wait(pe, h_lo_ready, HB * g + hb + 1)
                        last = nc.tensor.matmul(acc, h[:, hb, nodes_b], w[:, hb], start=(hb == 0 and i == 0),
                                                stop=(hb == HB - 1 and i == 2))
                last.then_inc(v_done, 1)

            def mix(k, off, b):
                g, p, q = grp(k, off), off % 2, b // 2
                if b % 2 == 0:
                    wait(pe, v_hi_ready, 2 * g + q + 1)
                    wait(pe, z_ready, 2 * g + q)
                    wait(pe, at_lo_ready, g + 1)
                terms = [(at_hi, v_hi), (at_lo, v_hi), (at_hi, v_lo)]
                for i, (a, v) in enumerate(terms):
                    if b % 2 == 0 and i == len(terms) - 1:
                        wait(pe, v_lo_ready, 2 * g + q + 1)
                    last = nc.tensor.matmul(ps_y[:, (b % 2) * d_in:(b % 2 + 1) * d_in], a[:, p, b], v[:, b],
                                            start=(i == 0), stop=(i == len(terms) - 1))
                last.then_inc(y_done, 1)

            def stay_warm(products):
                for _ in range(products):
                    nc.tensor.matmul(ps_hid[0][:, 0:P], ident[:, :], ident[:, :], start=True, stop=True)

            pe.wait_ge(consts, 2)
            stay_warm(5)
            turn_incidence(0, 0)
            pe.wait_ge(first_rows_in, 16)
            nc.tensor.transpose(ps_edge[:, 0:graphs], first_rows[:, :], ident[:, :]).then_inc(edge_turned, 1)
            pe.wait_ge(w1_in, 16)
            for db in range(DB):
                for hb in range(HB):
                    last = nc.tensor.transpose(ps_w[db][:, hb * P:(hb + 1) * P],
                                               w1_rows[:, hb, db * P:(db + 1) * P], ident[:, :])
            last.then_inc(w1_turned, 1)
            sums(0, 0)
            stay_warm(8)
            turn_scaled(0, 0)
            stay_warm(8)
            pe.wait_ge(edge_split, 1)
            make_at(0, 0)
            pe.wait_ge(b1_in, 16)
            nc.tensor.transpose(ps_rows[:, 0:HB], b1_rows[:, :], ident[0:HB, 0:HB]
                                ).then_inc(b1_turned, 1)
            stay_warm(5)
            make_u(0, 0)
            turn_incidence(0, 1)
            pe.wait_ge(w1_lo_ready, DB)
            pe.wait_ge(w2_centring, 2 + DB)
            for hb in range(HB):
                for db in range(DB):
                    at = (hb % 2) * d_in + db * P
                    last = nc.tensor.transpose(ps_w[hb // 2][:, at:at + P],
                                               w2_centred[:, db, hb * P:(hb + 1) * P], ident[:, :])
            last.then_inc(w2_turned, 1)

            def spread_t():
                pe.wait_ge(t_prep, 2 * DB + 1)
                pe.wait_ge(b1_ready, 1)
                for db in range(DB):
                    last = nc.tensor.matmul(ps_rows[:, db * P:(db + 1) * P], t_wide[:, db], ident[:, :],
                                            start=True, stop=True)
                last.then_inc(t_spread, 1)

            def first_iteration(k, off):
                hidden(k, off, 0)
                sums(k, off + 1)
                hidden(k, off, 1)
                hidden(k, off, 2)
                turn_scaled(k, off + 1)
                hidden(k, off, 3)
                pe.wait_ge(w2_lo_ready, 2)
                turn_h(k, off, 0)
                make_at(k, off + 1)
                second(k, off, 0)
                second(k, off, 1)
                turn_h(k, off, 1)
                turn_incidence(k, off + 2)
                make_u(k, off + 1)
                turn_h(k, off, 2)
                sums(k, off + 2)
                turn_h(k, off, 3)
                second(k, off, 2)
                spread_t()
                second(k, off, 3)

            def iteration(k, off, first, last):
                if first:
                    first_iteration(k, off)
                    return
                if not last:
                    turn_scaled(k, off + 1)
                hidden(k, off, 0)
                hidden(k, off, 1)
                mix(k, off - 1, 0)
                if not last:
                    make_at(k, off + 1)
                mix(k, off - 1, 1)
                hidden(k, off, 2)
                hidden(k, off, 3)
                mix(k, off - 1, 2)
                mix(k, off - 1, 3)
                turn_h(k, off, 0)
                turn_h(k, off, 1)
                if last:
                    for b in range(G4):
                        second(k, off, b)
                        if b + 2 < G4:
                            turn_h(k, off, b + 2)
                    return
                if not before_last(k, off):
                    turn_incidence(k, off + 2)
                make_u(k, off + 1)
                turn_h(k, off, 2)
                if not before_last(k, off):
                    sums(k, off + 2)
                turn_h(k, off, 3)
                for b in range(G4):
                    second(k, off, b)

            over_groups(pe, iteration)
            for b in range(G4):
                mix(PAIRS - 1, 1, b)


_INS = ["x", "adj", "L0_gnn_W1", "L0_gnn_b1", "L0_gnn_gamma", "L0_gnn_beta", "L0_gnn_W2", "L0_gnn_b2"]


def kernel(**inputs):
    import numpy as np
    import concourse.bacc as bacc
    from concourse.bass_utils import run_bass_kernel_spmd as run

    nc = bacc.Bacc("TRN2", target_bir_lowering=False, num_devices=1)
    arrays, args = {}, []
    for name in _INS:
        a = np.ascontiguousarray(inputs[name])
        arrays[f"in_{name}"] = a
        args.append(nc.dram_tensor(f"in_{name}", a.shape, mybir.dt.from_np(a.dtype), kind="ExternalInput").ap())
    out = nc.dram_tensor("out", arrays["in_x"].shape, F32, kind="ExternalOutput").ap()
    hypergraph_block(nc, *args, out)
    r = run(nc, [arrays], core_ids=[0])
    return r.results[0]["out"]
```
